# Optimizing a Trainium2 kernel written in Bass

```python
import numpy as np
import jax
import jax.numpy as jnp

def _softmax(x, axis=-1):
    return jax.nn.softmax(x, axis=axis)

def _gelu(x):
    return jax.nn.gelu(x, approximate=True)

def _silu(x):
    return jax.nn.silu(x)

def _sigmoid(x):
    return jax.nn.sigmoid(x)

def _layernorm(x, axis=-1, eps=1e-05):
    m = jnp.mean(x, axis=axis, keepdims=True)
    v = jnp.var(x, axis=axis, keepdims=True)
    return (x - m) / jnp.sqrt(v + eps)

def _scatter_add(tgt, idx, src, axis=0):
    return tgt.at[idx].add(src)

def _segment_sum(src, seg, n):
    return jax.ops.segment_sum(src, seg, n)
kernel_name = 'mk_conv_preact_d2_conv_nchw512_r2_31fa46'

def setup_inputs(seed: int=0):
    np.random.seed(seed)
    _w = jnp.asarray

    def _rec_inputs():
        import jax
        import jax.numpy as jnp
        _gk = jax.random.key(seed)
        x = -0.0003929 + 0.9999 * jax.random.normal(jax.random.fold_in(_gk, 1), (8, 256, 32, 32), jnp.float32)
        return x
    x = _rec_inputs()

    def _L0_conv_setup():
        import jax, jax.numpy as jnp
        import numpy as np
        from jax import lax
        K = 5
        WIN = (1, 1, K, K)
        PAD = ((0, 0), (0, 0), (K // 2, K // 2), (K // 2, K // 2))
        T_POOL = 0.9

        def _conv(x, w, b, pad, dil=(1, 1), groups=1):
            y = lax.conv_general_dilated(x, w, (1, 1), pad, rhs_dilation=dil, dimension_numbers=('NCHW', 'OIHW', 'NCHW'), feature_group_count=groups)
            return y + b[None, :, None, None]

        def _cbs(x, w, b):
            return jax.nn.silu(_conv(x, w, b, ((0, 0), (0, 0))))

        def _maxpool(x):
            return lax.reduce_window(x, -jnp.inf, lax.max, WIN, (1, 1, 1, 1), PAD)

        def _sumpool(x):
            return lax.reduce_window(x, 0.0, lax.add, WIN, (1, 1, 1, 1), PAD)

        def _tmaxavg(x):
            return T_POOL * _maxpool(x) + (1.0 - T_POOL) * (_sumpool(x) / (K * K))

        def _rwpool(x):
            c = lax.stop_gradient(jnp.max(x))
            e = jnp.exp(x - c)
            return _sumpool(e * x) / (_sumpool(e) + 1e-06)
        key = jax.random.key(seed)
        ks = jax.random.split(key, 16)
        B, C1, H, W = (8, 256, 32, 32)
        c_ = C1 // 2
        c4 = c_ * 4
        C2 = 256
        f32 = jnp.float32

        def w(k, shape):
            return jax.random.normal(k, shape, f32) * 0.02
        return {'x': jax.random.normal(ks[0], (B, C1, H, W), f32), 'w_sta': w(ks[1], (c_, C1, 1, 1)), 'b_sta': jnp.zeros((c_,), f32), 'w_cv1': w(ks[2], (C2, c4, 1, 1)), 'b_cv1': jnp.zeros((C2,), f32), 'w_cv2': w(ks[3], (C2, c4, 1, 1)), 'b_cv2': jnp.zeros((C2,), f32), 'w_cvend': w(ks[4], (C2, c4, 1, 1)), 'b_cvend': jnp.zeros((C2,), f32), 'w_dwh': w(ks[5], (c4, 1, 1, 3)), 'b_dwh': jnp.zeros((c4,), f32), 'w_dwv': w(ks[6], (c4, 1, 3, 1)), 'b_dwv': jnp.zeros((c4,), f32), 'w_ddwh': w(ks[7], (c4, 1, 1, 3)), 'b_ddwh': jnp.zeros((c4,), f32), 'w_ddwv': w(ks[8], (c4, 1, 3, 1)), 'b_ddwv': jnp.zeros((c4,), f32), 'w_c1': w(ks[9], (c4, c4, 1, 1)), 'b_c1': jnp.zeros((c4,), f32)}
    _L0_conv_all = _L0_conv_setup()
    _L0_conv_in = {k: v for k, v in _L0_conv_all.items() if k in ('w_sta', 'b_sta', 'w_cv1', 'b_cv1', 'w_cv2', 'b_cv2', 'w_cvend', 'b_cvend', 'w_dwh', 'b_dwh', 'w_dwv', 'b_dwv', 'w_ddwh', 'b_ddwh', 'w_ddwv', 'b_ddwv', 'w_c1', 'b_c1')}
    del _L0_conv_all

    def _L1_conv_setup():
        import jax, jax.numpy as jnp
        import numpy as np
        DIM = 256
        key = jax.random.key(seed)
        k1, k2, k3 = jax.random.split(key, 3)
        x = jax.random.normal(k1, (4, DIM, 32, 32), dtype=jnp.float32)
        w1 = jax.random.normal(k2, (DIM, DIM), dtype=jnp.float32) * DIM ** (-0.5)
        w2 = jax.random.normal(k3, (DIM, DIM), dtype=jnp.float32) * DIM ** (-0.5)
        return {'x': x, 'w1': w1, 'w2': w2}
    _L1_conv_all = _L1_conv_setup()
    _L1_conv_in = {k: v for k, v in _L1_conv_all.items() if k in ('w1', 'w2')}
    del _L1_conv_all
    return {'x': x, 'L0_conv_w_sta': _L0_conv_in['w_sta'], 'L0_conv_b_sta': _L0_conv_in['b_sta'], 'L0_conv_w_cv1': _L0_conv_in['w_cv1'], 'L0_conv_b_cv1': _L0_conv_in['b_cv1'], 'L0_conv_w_cv2': _L0_conv_in['w_cv2'], 'L0_conv_b_cv2': _L0_conv_in['b_cv2'], 'L0_conv_w_cvend': _L0_conv_in['w_cvend'], 'L0_conv_b_cvend': _L0_conv_in['b_cvend'], 'L0_conv_w_dwh': _L0_conv_in['w_dwh'], 'L0_conv_b_dwh': _L0_conv_in['b_dwh'], 'L0_conv_w_dwv': _L0_conv_in['w_dwv'], 'L0_conv_b_dwv': _L0_conv_in['b_dwv'], 'L0_conv_w_ddwh': _L0_conv_in['w_ddwh'], 'L0_conv_b_ddwh': _L0_conv_in['b_ddwh'], 'L0_conv_w_ddwv': _L0_conv_in['w_ddwv'], 'L0_conv_b_ddwv': _L0_conv_in['b_ddwv'], 'L0_conv_w_c1': _L0_conv_in['w_c1'], 'L0_conv_b_c1': _L0_conv_in['b_c1'], 'L1_conv_w1': _L1_conv_in['w1'], 'L1_conv_w2': _L1_conv_in['w2']}

def reference(x, L0_conv_w_sta, L0_conv_b_sta, L0_conv_w_cv1, L0_conv_b_cv1, L0_conv_w_cv2, L0_conv_b_cv2, L0_conv_w_cvend, L0_conv_b_cvend, L0_conv_w_dwh, L0_conv_b_dwh, L0_conv_w_dwv, L0_conv_b_dwv, L0_conv_w_ddwh, L0_conv_b_ddwh, L0_conv_w_ddwv, L0_conv_b_ddwv, L0_conv_w_c1, L0_conv_b_c1, L1_conv_w1, L1_conv_w2):
    import jax
    import jax.numpy as jnp

    def _L0_conv_ref(x, w_sta, b_sta, w_cv1, b_cv1, w_cv2, b_cv2, w_cvend, b_cvend, w_dwh, b_dwh, w_dwv, b_dwv, w_ddwh, b_ddwh, w_ddwv, b_ddwv, w_c1, b_c1):
        import jax, jax.numpy as jnp
        import numpy as np
        from jax import lax
        K = 5
        WIN = (1, 1, K, K)
        PAD = ((0, 0), (0, 0), (K // 2, K // 2), (K // 2, K // 2))
        T_POOL = 0.9

        def _conv(x, w, b, pad, dil=(1, 1), groups=1):
            y = lax.conv_general_dilated(x, w, (1, 1), pad, rhs_dilation=dil, dimension_numbers=('NCHW', 'OIHW', 'NCHW'), feature_group_count=groups)
            return y + b[None, :, None, None]

        def _cbs(x, w, b):
            return jax.nn.silu(_conv(x, w, b, ((0, 0), (0, 0))))

        def _maxpool(x):
            return lax.reduce_window(x, -jnp.inf, lax.max, WIN, (1, 1, 1, 1), PAD)

        def _sumpool(x):
            return lax.reduce_window(x, 0.0, lax.add, WIN, (1, 1, 1, 1), PAD)

        def _tmaxavg(x):
            return T_POOL * _maxpool(x) + (1.0 - T_POOL) * (_sumpool(x) / (K * K))

        def _rwpool(x):
            c = lax.stop_gradient(jnp.max(x))
            e = jnp.exp(x - c)
            return _sumpool(e * x) / (_sumpool(e) + 1e-06)
        x_aux = _cbs(x, w_sta, b_sta)
        y1 = [x_aux]
        y2 = [x_aux]
        for _ in range(3):
            y1.append(_tmaxavg(y1[-1]))
            y2.append(_rwpool(y2[-1]))
        y = jnp.concatenate([_cbs(jnp.concatenate(y1, 1), w_cv1, b_cv1), _cbs(jnp.concatenate(y2, 1), w_cv2, b_cv2)], 1)
        C = y.shape[1]
        a = _conv(y, w_dwh, b_dwh, ((0, 0), (1, 1)), groups=C)
        a = _conv(a, w_dwv, b_dwv, ((1, 1), (0, 0)), groups=C)
        a = _conv(a, w_ddwh, b_ddwh, ((0, 0), (2, 2)), dil=(1, 2), groups=C)
        a = _conv(a, w_ddwv, b_ddwv, ((2, 2), (0, 0)), dil=(2, 1), groups=C)
        a = _conv(a, w_c1, b_c1, ((0, 0), (0, 0)))
        return _cbs(y * a, w_cvend, b_cvend)

    def _L1_conv_ref(x, w1, w2):
        import jax, jax.numpy as jnp
        import numpy as np
        DIM = 256
        b, c, h, w = x.shape
        scale = c ** (-0.5)
        f = x.reshape(b, c, h * w).transpose(0, 2, 1)
        q = jnp.einsum('bnc,dc->bnd', f, w1)
        attn = jnp.einsum('bnd,bmd->bnm', q, f) * scale
        attn = jax.nn.softmax(attn, axis=-1)
        v = jnp.einsum('bnc,dc->bnd', f, w2)
        mixed = jnp.einsum('bnm,bmd->bnd', attn, v)
        return mixed.transpose(0, 2, 1).reshape(b, c, h, w)

    def _gn(v, G=32, eps=1e-05):
        B_, C_, H_, W_ = v.shape
        g = v.reshape(B_, G, C_ // G, H_, W_)
        m = jnp.mean(g, axis=(2, 3, 4), keepdims=True)
        s = jnp.var(g, axis=(2, 3, 4), keepdims=True)
        return ((g - m) / jnp.sqrt(s + eps)).reshape(v.shape)

    def _ln_c(v, eps=1e-06):
        m = jnp.mean(v, axis=1, keepdims=True)
        s = jnp.var(v, axis=1, keepdims=True)
        return (v - m) / jnp.sqrt(s + eps)

    def _ln_t(v, eps=1e-05):
        m = jnp.mean(v, axis=-1, keepdims=True)
        s = jnp.var(v, axis=-1, keepdims=True)
        return (v - m) / jnp.sqrt(s + eps)

    def _to_tokens(v):
        B_, C_, H_, W_ = v.shape
        return v.reshape(B_, C_, H_ * W_).transpose(0, 2, 1)

    def _from_tokens(t, like):
        B_, C_, H_, W_ = like.shape
        return t.transpose(0, 2, 1).reshape(B_, C_, H_, W_)
    x = x + _L0_conv_ref(_gn(x), L0_conv_w_sta, L0_conv_b_sta, L0_conv_w_cv1, L0_conv_b_cv1, L0_conv_w_cv2, L0_conv_b_cv2, L0_conv_w_cvend, L0_conv_b_cvend, L0_conv_w_dwh, L0_conv_b_dwh, L0_conv_w_dwv, L0_conv_b_dwv, L0_conv_w_ddwh, L0_conv_b_ddwh, L0_conv_w_ddwv, L0_conv_b_ddwv, L0_conv_w_c1, L0_conv_b_c1)
    x = x + _L1_conv_ref(_gn(x), L1_conv_w1, L1_conv_w2)
    return x

_drawn_inputs = setup_inputs


def setup_inputs(seed=0):
    import zlib

    import numpy as np

    out = dict(_drawn_inputs(seed))
    spreads = {'L0_conv_b_sta': (0.0, 0.8),
     'L0_conv_b_cv1': (0.0, 0.8),
     'L0_conv_b_cv2': (0.0, 0.8),
     'L0_conv_b_cvend': (0.0, 2.0),
     'L0_conv_b_dwh': (0.0, 2.0),
     'L0_conv_b_dwv': (0.0, 0.8),
     'L0_conv_b_ddwh': (0.0, 0.8),
     'L0_conv_b_ddwv': (0.0, 0.8),
     'L0_conv_b_c1': (0.0, 0.8)}
    factors = {'L0_conv_w_sta': 8.0,
     'L0_conv_w_cv1': 8.0,
     'L0_conv_w_cv2': 8.0,
     'L0_conv_w_cvend': 8.0,
     'L0_conv_w_dwh': 8.0,
     'L0_conv_w_dwv': 8.0,
     'L0_conv_w_ddwh': 8.0,
     'L0_conv_w_ddwv': 8.0,
     'L0_conv_w_c1': 8.0,
     'L1_conv_w1': 30.069,
     'L1_conv_w2': 5.953}
    for name, (base, spread) in spreads.items():
        noise = np.random.default_rng([zlib.crc32(name.encode()), seed]).standard_normal(out[name].shape)
        drawn = base * np.exp(spread * noise) if base else spread * noise
        out[name] = jnp.asarray(drawn.astype(out[name].dtype))
    for name, factor in factors.items():
        out[name] = (out[name] * factor).astype(out[name].dtype)
    return out
```

```python
import concourse.bass as bass
from concourse import mybir
from contextlib import ExitStack

F32 = mybir.dt.float32
F32R = mybir.dt.float32r
ALU = mybir.AluOpType
ACT = mybir.ActivationFunctionType
AX = mybir.AxisListType.X
RMAX = bass.bass_isa.ReduceOp.max

P = 128
B = 8
C = 256
CT = C // P
H = W = 32
N = H * W
HALF = 512
C4 = 512
KT = C4 // P
LEVELS = 3
WP = W + 4
GROUP = C // 32
T_POOL = 0.9
K2 = 25
LOWEST = -3.4028235e38
STAGES = 4
COLUMNS = {"b_sta": 1, "b_cv1": CT, "b_cv2": CT, "b_cvend": CT, "b_c1": KT,
           "taps": STAGES * KT * 3, "b_taps": STAGES * KT}
EXP_LN = "natural_log_exp_and_others"


class Signal:

    def __init__(self, sem, per):
        self.sem, self.per = sem, per

    def at(self, image, k):
        return image * self.per + k


class Steps:

    def __init__(self, eng, counted, image):
        self.eng, self.counted, self.image, self.k = eng, counted, image, 0

    def did(self, ins):
        self.k += 1
        ins.then_inc(self.counted.sem, 1)

    def wait(self):
        self.eng.wait_ge(self.counted.sem, self.counted.at(self.image, self.k))


def phase_a(nc, x, w, consts, keep, levels, rmc):
    with ExitStack() as ctx:
        def sb(name, shape, dt=F32):
            return ctx.enter_context(nc.sbuf_tensor(name, shape, dt))

        def sem(name):
            return ctx.enter_context(nc.semaphore(name))

        x_all = sb("x_all", [P, B, CT, N])
        xn = sb("xn", [P, 2, CT, N])
        stem = sb("stem", [P, 2, N])
        w_sta = sb("w_sta", [P, CT, P])
        w_attn = sb("w_attn", [P, 2, CT, C])
        stats = sb("stats", [P, B, CT, 2, 6])
        mv = sb("mv", [P, B * CT, 2])
        dev = sb("dev", [P, B * CT])
        spread = sb("spread", [P, B * CT])
        rstd = sb("rstd", [P, B * CT])
        shift = sb("shift", [P, B * CT])
        ps = ctx.enter_context(nc.psum_tensor("ps_a", [P, 2, N], F32))
        ps_mean = ctx.enter_context(nc.psum_tensor("ps_mean", [P, HALF], F32))
        ps_var = ctx.enter_context(nc.psum_tensor("ps_var", [P, HALF], F32))

        x_in = [sem(f"a_x_in{i}") for i in range(B)]
        weights_in = sem("a_weights_in")
        stats_done = sem("a_stats_done")
        mv_done = sem("a_mv_done")
        mean_done = sem("a_mean_done")
        dev_done = sem("a_dev_done")
        var_done = sem("a_var_done")
        eps_done = sem("a_eps_done")
        rstd_done = sem("a_rstd_done")
        shift_done = sem("a_shift_done")
        split_done = sem("a_split_done")
        xn_done = sem("a_xn_done")
        sta_done = sem("a_sta_done")
        stem_done = sem("a_stem_done")
        max_done = sem("a_max_done")
        stored = [sem(f"a_stored{u}") for u in range(2)]
        block = ctx.enter_context(nc.Block())

        x_v = x.rearrange("b (t p) h w -> b p t (h w)", p=P)

        @block.sync
        def _(sp):
            for i in range(B):
                sp.dma_start(x_all[:, i], x_v[i]).then_inc(x_in[i], 16)
            for u in range(2):
                sp.sem_inc(stored[u], 16)
            with sp.Fori(0, B // 2) as pair:
                for u in range(2):
                    n = pair * 2 + u
                    sp.wait_ge(stem_done, n + 3)
                    sp.dma_start(levels[n], stem[:, u]).then_inc(stored[u], 16)
            for u in range(2):
                sp.wait_ge(stored[u], 16 * (B // 2 + 1))

        @block.scalar
        def _(act):
            loads = [(keep[k][:, :], consts[k]) for k in ("ident", "group")]
            loads += [(w_sta[:, :, :], w["sta"].rearrange("(t p) o -> p t o", p=P)),
                      (w_attn[:, 0], w["w1"].rearrange("(t p) o -> p t o", p=P)),
                      (w_attn[:, 1], w["w2"].rearrange("(t p) o -> p t o", p=P))]
            loads += [(keep[k][:, :, :], w[k].rearrange("(t p) o -> p t o", p=P)) for k in ("cv1", "cv2", "cvend", "c1")]
            loads.append((keep["columns"][:, :], w["columns"]))
            for dst, src in loads:
                act.dma_start(dst, src).then_inc(weights_in, 16)
            act.wait_ge(weights_in, 16 * len(loads))
            act.sem_inc(stem_done, 2)
            with act.Fori(0, B // 2) as pair:
                for u in range(2):
                    n = pair * 2 + u
                    act.wait_ge(sta_done, n + 3)
                    act.wait_ge(max_done, n + 1)
                    act.wait_ge(stored[u], 16 * pair + 16)
                    nc.scalar.activation(stem[:, u], ps[:, u], ACT.Silu, bias=keep["b_sta"]).then_inc(stem_done, 1)

        @block.tensor
        def _(pe):
            pe.sem_inc(sta_done, 2)
            pe.wait_ge(stem_done, 2)
            pe.wait_ge(mv_done, B * CT)
            nc.tensor.matmul(ps_mean[:, 0:B * CT], keep["group"][:, :], mv[:, :, 0], start=True, stop=True).then_inc(mean_done, 1)
            pe.wait_ge(dev_done, 3)
            nc.tensor.matmul(ps_var[:, 0:B * CT], keep["group"][:, :], spread[:, :], start=True, stop=True).then_inc(var_done, 1)
            with pe.Fori(0, B // 2) as pair:
                for u in range(2):
                    n = pair * 2 + u
                    pe.wait_ge(xn_done, CT * n + CT)
                    pe.wait_ge(stem_done, n + 1)
                    for h in range(2):
                        for k in range(CT):
                            last = nc.tensor.matmul(ps[:, u, h * HALF:(h + 1) * HALF], w_sta[:, k, :],
                                                    xn[:, u, k, h * HALF:(h + 1) * HALF], start=(k == 0), stop=(k == CT - 1))
                    last.then_inc(sta_done, 1)

        @block.gpsimd
        def _(pool):
            nc.gpsimd.memset(keep["minus_half"][:, :], -0.5).then_inc(rstd_done, 1)
            pool.wait_ge(rstd_done, 1)
            pool.wait_ge(eps_done, 1)
            nc.gpsimd.tensor_tensor(rstd[:, :], spread[:, :], keep["minus_half"][:, :], ALU.pow).then_inc(rstd_done, 1)

        @block.vector
        def _(dve):
            for i in range(B):
                dve.wait_ge(x_in[i], 16)
                for t in range(CT):
                    for h in range(2):
                        nc.vector.bn_stats(stats[:, i, t, h, :], x_all[:, i, t, h * HALF:(h + 1) * HALF]).then_inc(stats_done, 1)
            dve.wait_ge(stats_done, B * CT * 2)
            for i in range(B):
                for t in range(CT):
                    nc.vector.bn_aggr(mv[:, i * CT + t, :], stats[:, i, t].rearrange("p h s -> p (h s)")).then_inc(mv_done, 1)
            dve.wait_ge(mean_done, 1)
            dve.wait_ge(mv_done, B * CT)
            nc.vector.tensor_tensor(dev[:, :], mv[:, :, 0], ps_mean[:, 0:B * CT], ALU.subtract).then_inc(dev_done, 1)
            dve.wait_ge(dev_done, 1)
            nc.vector.tensor_tensor(dev[:, :], dev[:, :], dev[:, :], ALU.mult).then_inc(dev_done, 1)
            dve.wait_ge(dev_done, 2)
            nc.vector.tensor_tensor(spread[:, :], dev[:, :], mv[:, :, 1], ALU.add).then_inc(dev_done, 1)
            dve.wait_ge(stem_done, 2)
            for n, name in enumerate(("w1", "w2")):
                nc.vector.tensor_copy(keep[name + "_hi"][:, :, :], w_attn[:, n]).then_inc(split_done, 1)
                dve.wait_ge(split_done, 2 * n + 1)
                nc.vector.tensor_tensor(keep[name + "_lo"][:, :, :], w_attn[:, n], keep[name + "_hi"][:, :, :].bitcast(F32),
                                        ALU.subtract).then_inc(split_done, 1)
            dve.wait_ge(var_done, 1)
            nc.vector.tensor_scalar(spread[:, :], ps_var[:, 0:B * CT], 1e-5, None, ALU.add).then_inc(eps_done, 1)
            dve.wait_ge(rstd_done, 2)
            nc.vector.scalar_tensor_tensor(shift[:, :], ps_mean[:, 0:B * CT], -1.0, rstd[:, :], ALU.mult, ALU.mult).then_inc(shift_done, 1)
            dve.wait_ge(shift_done, 1)
            dve.sem_inc(max_done, 2)

            def normalise(n, u):
                dve.wait_ge(sta_done, n + 1)
                for t in range(CT):
                    nc.vector.tensor_scalar(xn[:, u, t], x_all[:, n, t], rstd[:, bass.ds(n * CT + t, 1)],
                                            shift[:, bass.ds(n * CT + t, 1)], ALU.mult, ALU.add).then_inc(xn_done, 1)

            def maximum(n, u):
                dve.wait_ge(stem_done, n + 3)
                nc.vector.reduce_max(rmc[:, bass.ds(n, 1)], stem[:, u], AX).then_inc(max_done, 1)

            normalise(0, 0)
            normalise(1, 1)
            with dve.Fori(0, B // 2 - 1) as pair:
                for u in range(2):
                    maximum(pair * 2 + u, u)
                    normalise(pair * 2 + u + 2, u)
            maximum(B - 2, 0)
            maximum(B - 1, 1)


def phase_b(nc, consts, keep, levels, rmc):
    with ExitStack() as ctx:
        def sb(name, shape, dt=F32):
            return ctx.enter_context(nc.sbuf_tensor(name, shape, dt))

        def sem(name):
            return ctx.enter_context(nc.semaphore(name))

        box = sb("box", [P, 8 * W])
        y_in = sb("y_in", [P, 2, N])
        e = sb("e", [P, 2, N])
        ey = sb("ey", [P, 2, N])
        r = sb("r", [P, 2, N])
        newton = sb("newton", [P, 2, N])
        y_out = sb("y_out", [P, 2, N])
        tile_max = sb("tile_max", [P, 1])
        batch_max = sb("batch_max", [P, 1])
        minus_max = sb("minus_max", [P, 1])
        eps = sb("eps", [P, 1])
        ps_t = ctx.enter_context(nc.psum_tensor("ps_t", [P, 2, N], F32))
        ps_e = ctx.enter_context(nc.psum_tensor("ps_e", [P, N], F32))
        ps_ey = ctx.enter_context(nc.psum_tensor("ps_ey", [P, N], F32))

        box_in = sem("b_box_in")
        loaded = [sem(f"b_loaded{u}") for u in range(2)]
        turned = sem("b_turned")
        exp_done = sem("b_exp_done")
        ey_done = sem("b_ey_done")
        sum_e_done = sem("b_sum_e_done")
        sum_ey_done = sem("b_sum_ey_done")
        r_done = sem("b_r_done")
        newton_done = sem("b_newton_done")
        y_done = sem("b_y_done")
        col_max_done = sem("b_col_max_done")
        tile_max_done = sem("b_tile_max_done")
        batch_max_done = sem("b_batch_max_done")
        minus_max_done = sem("b_minus_max_done")
        eps_set = sem("b_eps_set")
        gate = sem("b_gate")
        stored = [sem(f"b_stored{u}") for u in range(2)]
        block = ctx.enter_context(nc.Block())

        def images(eng, head, full, sixth, last):
            with eng.Fori(0, LEVELS) as level:
                head(level)
                with eng.Fori(0, B // 2 - 1) as pair:
                    for u in range(2):
                        full(level * (B // 2) + pair, pair * 2 + u, u)
                sixth(level * (B // 2) + B // 2 - 1, B - 2, 0)
                last(level * (B // 2) + B // 2 - 1, B - 1, 1)

        @block.sync
        def _(sp):
            sp.dma_start(box[:, :], consts["box"]).then_inc(box_in, 16)

            def load(q, u):
                n = q * 2 + u
                sp.wait_ge(turned, n + 1)
                sp.wait_ge(stored[u], q * 16 + 16)
                sp.dma_start(y_in[:, u], levels[n]).then_inc(loaded[u], 16)

            def store(q, m, u):
                n = q * 2 + u
                sp.wait_ge(y_done, n + 2)
                sp.dma_start(levels[n + B], y_out[:, u]).then_inc(stored[u], 16)

            def head(level):
                load(level * (B // 2), 0)
                load(level * (B // 2), 1)

            def full(q, m, u):
                load(q + 1, u)
                store(q, m, u)

            for u in range(2):
                sp.sem_inc(stored[u], 16 * (B // 2))
            images(sp, head, full, store, store)
            for u in range(2):
                sp.wait_ge(stored[u], 16 * (B // 2) * (LEVELS + 1))

        @block.tensor
        def _(pe):
            def turn(q, u):
                n = q * 2 + u
                pe.wait_ge(loaded[u], q * 16 + 16)
                pe.wait_ge(ey_done, n + 1)
                for k in range(N // P):
                    last = nc.tensor.transpose(ps_t[:, u, k * P:(k + 1) * P], y_in[:, u, k * P:(k + 1) * P], keep["ident"][:, :])
                last.then_inc(turned, 1)

            def box_sum(out, pixels):
                rows, bank = P // W, HALF // W
                started = set()
                for k in range(N // P):
                    lo, hi = max(rows * k - 2, 0), min(rows * k + rows + 2, H)
                    for b in range(lo // bank, (hi - 1) // bank + 1):
                        r0, r1 = max(lo, b * bank), min(hi, (b + 1) * bank)
                        c0 = (r0 - (rows * k - 2)) * W
                        last = nc.tensor.matmul(out[:, r0 * W:r1 * W], pixels[:, k * P:(k + 1) * P],
                                                box[:, c0:c0 + (r1 - r0) * W], start=(b not in started),
                                                stop=(k == N // P - 1), skip_group_check=True)
                        started.add(b)
                return last

            def sums(q, m, u):
                n = q * 2 + u
                pe.wait_ge(exp_done, n + 1)
                pe.wait_ge(newton_done, n * 2 + 1)
                box_sum(ps_e, e[:, u]).then_inc(sum_e_done, 1)
                pe.wait_ge(ey_done, n + 3)
                pe.wait_ge(y_done, n + 1)
                box_sum(ps_ey, ey[:, u]).then_inc(sum_ey_done, 1)

            def full(q, m, u):
                turn(q + u, 1 - u)
                sums(q, m, u)

            pe.sem_inc(turned, 2)
            pe.sem_inc(sum_ey_done, 2)
            pe.wait_ge(box_in, 16)
            images(pe, lambda level: turn(level * (B // 2), 0), full, full, sums)

        @block.scalar
        def _(act):
            def exponent(q, u):
                n = q * 2 + u
                act.wait_ge(turned, n + 3)
                act.wait_ge(sum_ey_done, n + 1)
                nc.scalar.activation(e[:, u], ps_t[:, u], ACT.Exp, bias=minus_max[:, 0:1]).then_inc(exp_done, 1)

            def estimate(q, m, u):
                n = q * 2 + u
                act.wait_ge(sum_e_done, n + 1)
                nc.scalar.activation(r[:, u], ps_e[:, :], ACT.Ln, bias=eps[:, 0:1]).then_inc(r_done, 1)
                act.wait_ge(r_done, n * 2 + 1)
                nc.scalar.activation(r[:, u], r[:, u], ACT.Exp, scale=-1.0).then_inc(r_done, 1)

            def head(level):
                act.wait_ge(batch_max_done, level + 1)
                nc.scalar.mul(minus_max[:, :], batch_max[:, :], -1.0).then_inc(minus_max_done, 1)
                act.wait_ge(minus_max_done, level + 1)
                exponent(level * (B // 2), 0)

            def full(q, m, u):
                exponent(q + u, 1 - u)
                estimate(q, m, u)

            nc.scalar.preload_act_table_set(EXP_LN)
            act.wait_ge(eps_set, 1)
            images(act, head, full, full, estimate)

        @block.gpsimd
        def _(pool):
            nc.gpsimd.memset(eps[:, :], 1e-6).then_inc(eps_set, 1)
            with pool.Fori(0, LEVELS) as level:
                pool.wait_ge(tile_max_done, level + 1)
                pool.sem_inc(gate, 1)
                nc.gpsimd.partition_all_reduce(batch_max[:, :], tile_max[:, :], P, RMAX).then_inc(batch_max_done, 1)

        @block.vector
        def _(dve):
            def product(q, u):
                n = q * 2 + u
                dve.wait_ge(exp_done, n + 1)
                nc.vector.tensor_tensor(ey[:, u], ps_t[:, u], e[:, u], ALU.mult).then_inc(ey_done, 1)

            def divide(q, m, u):
                n = q * 2 + u
                dve.wait_ge(r_done, n * 2 + 2)
                nc.vector.scalar_tensor_tensor(newton[:, u], ps_e[:, :], 1e-6, r[:, u], ALU.add, ALU.mult).then_inc(newton_done, 1)
                dve.wait_ge(newton_done, n * 2 + 3)
                nc.vector.scalar_tensor_tensor(newton[:, u], newton[:, u], 2.0, r[:, u], ALU.subtract, ALU.mult).then_inc(newton_done, 1)
                dve.wait_ge(newton_done, n * 2 + 4)
                dve.wait_ge(sum_ey_done, n + 3)
                dve.wait_ge(stored[u], q * 16 + 16 * (B // 2))
                nc.vector.scalar_tensor_tensor(y_out[:, u], newton[:, u], -1.0, ps_ey[:, :], ALU.mult, ALU.mult).then_inc(y_done, 1)
                dve.wait_ge(y_done, n + 2)
                nc.vector.reduce_max(rmc[:, bass.ds(m, 1)], y_out[:, u], AX).then_inc(col_max_done, 1)

            def head(level):
                dve.wait_ge(col_max_done, level * B + 1)
                nc.vector.reduce_max(tile_max[:, :], rmc[:, :], AX).then_inc(tile_max_done, 1)
                product(level * (B // 2), 0)

            def full(q, m, u):
                product(q + u, 1 - u)
                divide(q, m, u)

            dve.sem_inc(ey_done, 2)
            dve.sem_inc(newton_done, 2)
            dve.sem_inc(y_done, 1)
            dve.sem_inc(col_max_done, 1)
            images(dve, head, full, full, divide)


def kept_tensors(ctx, nc):
    shapes = {"ident": [P, P], "group": [P, P], "cv1": [P, KT, C], "cv2": [P, KT, C], "cvend": [P, KT, C],
              "c1": [P, KT, C4], "columns": [P, sum(COLUMNS.values())], "minus_half": [P, B * CT]}
    keep = {k: ctx.enter_context(nc.sbuf_tensor("k_" + k, v, F32)) for k, v in shapes.items()}
    at = 0
    for k, n in COLUMNS.items():
        keep[k] = keep["columns"][:, at:at + n]
        at += n
    keep["taps"] = keep["taps"].rearrange("p (s t k) -> p s t k", s=STAGES, t=KT)
    keep["b_taps"] = keep["b_taps"].rearrange("p (s t) -> p s t", s=STAGES)
    for k in ("w1_hi", "w1_lo", "w2_hi", "w2_lo"):
        keep[k] = ctx.enter_context(nc.sbuf_tensor("k_" + k, [P, CT, C], F32R))
    return keep


def constants():
    import numpy as np

    ident = np.eye(P, dtype=np.float32)
    group = np.kron(np.eye(P // GROUP), np.full((GROUP, GROUP), 1.0 / GROUP)).astype(np.float32)
    near_x = np.abs(np.arange(W)[:, None] - np.arange(W)[None, :]) <= 2
    near_r = np.abs(np.arange(P // W)[:, None] + 2 - np.arange(8)[None, :]) <= 2
    return {"ident": ident, "group": group, "box": np.kron(near_r, near_x).astype(np.float32)}


def columns(inputs):
    import numpy as np

    def tiles(a):
        return a.reshape(-1, P).T

    cols = [tiles(inputs["L0_conv_b_" + k]) for k in ("sta", "cv1", "cv2", "cvend", "c1")]
    names = ("dwh", "dwv", "ddwh", "ddwv")
    cols += [inputs["L0_conv_w_" + k].reshape(KT, P, 3).transpose(1, 0, 2).reshape(P, -1) for k in names]
    cols += [tiles(inputs["L0_conv_b_" + k]) for k in names]
    return np.ascontiguousarray(np.concatenate(cols, axis=1))


MIX = 7
BEFORE, TILES = 6, N // P
ORDER = (2, 3, 0, 1)


def phase_c(nc, x, out, keep, levels):
    with ExitStack() as ctx:
        def sb(name, shape, dt=F32):
            return ctx.enter_context(nc.sbuf_tensor(name, shape, dt))

        def signal(name, per):
            return Signal(ctx.enter_context(nc.semaphore("c_" + name)), per)

        chain_in = sb("chain_in", [P, N])
        y2 = sb("y2", [P, LEVELS, N])
        wide = sb("wide", [P, LEVELS + 1, H, WP])
        zero = sb("zero", [P, H, WP])
        tall = sb("tall", [P, H + 4, W])
        tall_sum = sb("tall_sum", [P, H + 4, W])
        sum_a = sb("sum_a", [P, (H + 2) * W])
        sum_b = sb("sum_b", [P, H, W])
        work = sb("work", [P, 2, (H + 2) * W])
        y = sb("y", [P, KT, N])
        a = sb("a", [P, KT, N])
        x1 = sb("x1", [P, CT, N])
        f_hi = sb("f_hi", [P, CT, N], F32R)
        f_lo = sb("f_lo", [P, CT, N], F32R)
        q_hi = sb("q_hi", [P, CT, N], F32R)
        q_lo = sb("q_lo", [P, CT, N], F32R)
        v_hi = sb("v_hi", [P, N // P, C], F32R)
        v_lo = sb("v_lo", [P, N // P, C], F32R)
        prob = sb("prob", [P, N])
        pt_hi = sb("pt_hi", [P, 2, N], F32R)
        pt_lo = sb("pt_lo", [P, 2, N], F32R)
        mixed = sb("mixed", [P, 2, C])
        minus_max = sb("c_minus_max", [P, TILES])
        row_sum = sb("row_sum", [P, TILES])
        row_inv = sb("row_inv", [P, TILES])
        stats = sb("c_stats", [P, CT, 2, 6])
        mv = sb("c_mv", [P, CT, 2])
        gmean = sb("gmean", [P, CT])
        dev = sb("c_dev", [P, CT])
        spread = sb("c_spread", [P, CT])
        rstd = sb("c_rstd", [P, CT])
        shift = sb("c_shift", [P, CT])
        slots = [ctx.enter_context(nc.psum_tensor(f"slot{n}", [P, N], F32)) for n in range(3)]
        ps_o = ctx.enter_context(nc.psum_tensor("ps_o", [P, HALF], F32))
        ps_ot = ctx.enter_context(nc.psum_tensor("ps_ot", [P, HALF], F32))

        chain_loaded = signal("chain_loaded", 16)
        y2_loaded = signal("y2_loaded", 16)
        x_loaded = signal("x_loaded", 16)
        stored = signal("stored", 16)
        padded = signal("padded", 4)
        chain = signal("chain", MIX * LEVELS)
        summed = signal("summed", 6 * LEVELS)
        averaged = signal("averaged", LEVELS)
        cv = signal("cv", 2 * CT)
        y_ready = signal("y_ready", KT)
        centre = signal("centre", KT * STAGES)
        taps = signal("taps", 2 * KT * STAGES)
        c1 = signal("c1", KT)
        gated = signal("gated", KT)
        cvend = signal("cvend", CT)
        ended = signal("ended", CT)
        added = signal("added", CT)
        bn = signal("bn", 4 + CT)
        group_mean = signal("group_mean", 1)
        group_var = signal("group_var", 1)
        norm = signal("norm", 6)
        rstd_done = signal("rstd", 1)
        f_done = signal("f", CT)
        f_split = signal("f_split", 2 * CT)
        qv = signal("qv", 4)
        qv_hi = signal("qv_hi", 4)
        qv_lo = signal("qv_lo", 4)
        scores = signal("scores", TILES)
        maxed = signal("maxed", TILES)
        prob_done = signal("prob", TILES)
        turned = signal("turned", TILES)
        pt_hi_done = signal("pt_hi", TILES)
        pt_lo_done = signal("pt_lo", TILES)
        pv = signal("pv", TILES)
        inverse = signal("inverse", TILES)
        mixed_done = signal("mixed", TILES)
        back = signal("back", TILES)
        result = signal("result", TILES)
        ready = signal("ready", 0)
        stats_gate = ctx.enter_context(nc.semaphore("c_gate"))
        block = ctx.enter_context(nc.Block())

        x_v = x.rearrange("b (t p) h w -> b p t (h w)", p=P)
        out_v = out.rearrange("b (t p) h w -> b p t (h w)", p=P)
        y2_v = levels.rearrange("(l b) p n -> b p l n", b=B)

        def inner(k):
            return wide[:, k, :, 2:2 + W]

        def image2d(ap):
            return ap.rearrange("p (h w) -> p h w", w=W)

        def steps(eng, step):
            step(0, True, False, True)
            with eng.Fori(1, B - 1) as i:
                step(i, True, True, True)
            step(B - 1, True, True, False)
            step(B, False, True, False)

        def wait(eng, sig, image, k):
            eng.wait_ge(sig.sem, sig.at(image, k))

        def slot_uses(conv, attn):
            uses = [("cv", k) for k in range(2 * CT)] if conv else []
            if attn:
                uses += [("qv", k) for k in range(4)] + [("s", 0)]
                for t in range(TILES):
                    uses += [("s", t + 1)] * (t + 1 < TILES) + [("t", t)]
            return uses + ([("c1", k) for k in range(KT)] + [("ce", k) for k in range(CT)] if conv else [])

        def slot_plan(conv, attn):
            first = 1 if attn else 0
            return {use: slots[(first + n) % 3] for n, use in enumerate(slot_uses(conv, attn))}

        def stages_of(t):
            rest = KT * STAGES - BEFORE
            return range(BEFORE + rest * t // TILES, BEFORE + rest * (t + 1) // TILES)

        def stage(n):
            c, s = ORDER[n // STAGES], n % STAGES
            w0, w1 = work[:, 0, 0:N], work[:, 1, 0:N]
            src, dst = ((y[:, c], w0), (w0, w1), (w1, w0), (w0, a[:, c]))[s]
            return c, s, src, dst

        @block.sync
        def _(sp):
            def load_chain(i):
                sp.dma_start(chain_in[:, :], levels[i]).then_inc(chain_loaded.sem, 16)

            def load_y2(i):
                sp.dma_start(y2[:, :, :], y2_v[i, :, 1:LEVELS + 1]).then_inc(y2_loaded.sem, 16)

            def step(i, conv, attn, chained):
                if chained:
                    wait(sp, padded, i, 2)
                    load_chain(i + 1)
                    wait(sp, cv, i, CT)
                    load_y2(i + 1)
                if attn:
                    wait(sp, result, i - 1, TILES)
                    sp.dma_start(out_v[i - 1], x1[:, :, :]).then_inc(stored.sem, 16)
                    wait(sp, stored, i - 1, 16)
                if conv:
                    sp.dma_start(x1[:, :, :], x_v[i]).then_inc(x_loaded.sem, 16)

            load_chain(0)
            load_y2(0)
            steps(sp, step)

        @block.gpsimd
        def _(pool):
            nc.gpsimd.memset(zero[:, :, :], 0.0).then_inc(ready.sem, 1)
            nc.gpsimd.memset(tall_sum[:, :, :], 0.0).then_inc(ready.sem, 1)
            pool.wait_ge(ready.sem, 2 + 7)

            def box_sums(i, level, own):
                wait(pool, padded, i, 2 + level)
                sa = sum_a[:, :].rearrange("p (h w) -> p h w", w=WP - 2)
                sv = sum_a[:, :].rearrange("p (h w) -> p h w", w=W)

                def add(out, in0, in1):
                    own.did(nc.gpsimd.tensor_tensor(out, in0, in1, ALU.add))
                    own.wait()

                add(sa, zero[:, :, 0:WP - 2], zero[:, :, 1:WP - 1])
                add(sum_b[:, :, :], sa[:, :, 0:W], sa[:, :, 2:W + 2])
                add(tall_sum[:, 2:H + 2], sum_b[:, :, :], zero[:, :, 4:WP])
                add(sv, tall_sum[:, 0:H + 2], tall_sum[:, 1:H + 3])
                add(sum_b[:, :, :], sv[:, 0:H], sv[:, 2:H + 2])
                add(sum_b[:, :, :], sum_b[:, :, :], tall_sum[:, 4:H + 4])

            def pooling(i):
                own = Steps(pool, summed, i)
                for level in range(LEVELS):
                    box_sums(i, level, own)

            def step(i, conv, attn, chained):
                if attn:
                    wait(pool, norm, i - 1, 4)
                    nc.gpsimd.tensor_tensor(rstd[:, :], spread[:, :], keep["minus_half"][:, 0:CT], ALU.pow).then_inc(rstd_done.sem, 1)
                if chained:
                    wait(pool, chain, i, MIX * LEVELS)
                    pooling(i + 1)

            pooling(0)
            steps(pool, step)

        @block.tensor
        def _(pe):
            def released(use, i, own):
                kind, k = use
                image = i if own else i - 1
                return {"cv": (y_ready, image, k + 1), "c1": (gated, image, k + 1), "ce": (ended, image, k + 1),
                        "qv": (qv_lo, i - 1, k + 1), "s": (prob_done, i - 1, k + 1), "t": (pt_lo_done, i - 1, k + 1)}[kind]

            def step(i, conv, attn, chained):
                uses, slots_of = slot_uses(conv, attn), slot_plan(conv, attn)

                def claim(kind, k):
                    n = uses.index((kind, k))
                    if n >= 3:
                        wait(pe, *released(uses[n - 3], i, True))
                    elif attn:
                        wait(pe, *released(slot_uses(True, False)[n - 3], i, False))
                    return slots_of[kind, k]

                def product(kind, m, weights, inputs, sig):
                    slot = claim(kind, m)
                    for h in range(2):
                        for k in range(KT):
                            last = nc.tensor.matmul(slot[:, h * HALF:(h + 1) * HALF], weights[:, k], inputs(k, h),
                                                    start=(k == 0), stop=(k == KT - 1))
                    last.then_inc(sig.sem, 1)

                def cols(m):
                    return slice(m * P, (m + 1) * P)

                def flat(t):
                    return lambda k, h: t[:, k, h * HALF:(h + 1) * HALF]

                def cat2(k, h):
                    return y2[:, k - 1, h * HALF:(h + 1) * HALF] if k else cat1(k, h)

                def cat1(k, h):
                    return wide[:, k, h * (H // 2):(h + 1) * (H // 2), 2:2 + W]

                def split_product(out, pairs, last_signal=None):
                    parts = [(lh, rh) for lh, ll, rh, rl in pairs] + [(lh, rl) for lh, ll, rh, rl in pairs] \
                        + [(ll, rh) for lh, ll, rh, rl in pairs]
                    for n, (lhs, rhs) in enumerate(parts):
                        last = nc.tensor.matmul(out, lhs, rhs, start=(n == 0), stop=(n == len(parts) - 1))
                    return last

                def score(t):
                    wait(pe, qv_lo, i - 1, 2)
                    slot = claim("s", t)
                    for h in range(2):
                        hs = slice(h * HALF, (h + 1) * HALF)
                        last = split_product(slot[:, hs], [(q_hi[:, k, cols(t)], q_lo[:, k, cols(t)], f_hi[:, k, hs], f_lo[:, k, hs])
                                                           for k in range(CT)])
                    last.then_inc(scores.sem, 1)

                def turn(t):
                    wait(pe, prob_done, i - 1, t + 1)
                    slot = claim("t", t)
                    for m in range(N // P):
                        last = nc.tensor.transpose(slot[:, cols(m)], prob[:, cols(m)], keep["ident"][:, :])
                    last.then_inc(turned.sem, 1)

                def mix(t):
                    wait(pe, pt_lo_done, i - 1, t + 1)
                    wait(pe, qv_lo, i - 1, 4)
                    if t:
                        wait(pe, mixed_done, i - 1, t)
                    split_product(ps_o[:, 0:C], [(pt_hi[:, t % 2, cols(m)], pt_lo[:, t % 2, cols(m)], v_hi[:, m], v_lo[:, m])
                                                 for m in range(N // P)]).then_inc(pv.sem, 1)

                def turn_back(t):
                    wait(pe, mixed_done, i - 1, t + 1)
                    if t:
                        wait(pe, result, i - 1, t)
                    for d in range(CT):
                        last = nc.tensor.transpose(ps_ot[:, cols(d)], mixed[:, t % 2, cols(d)], keep["ident"][:, :])
                    last.then_inc(back.sem, 1)

                def group_sums(rhs, ps, sig):
                    nc.tensor.matmul(ps[:, 0:CT], keep["group"][:, :], rhs, start=True, stop=True).then_inc(sig.sem, 1)

                if conv:
                    wait(pe, y2_loaded, i, 16)
                    wait(pe, padded, i, 1)
                    product("cv", 0, keep["cv2"][:, :, cols(0)], cat2, cv)
                if attn:
                    wait(pe, bn, i - 1, 4 + CT)
                    group_sums(mv[:, :, 0], ps_o, group_mean)
                if conv:
                    product("cv", 1, keep["cv2"][:, :, cols(1)], cat2, cv)
                if attn:
                    wait(pe, norm, i - 1, 3)
                    group_sums(spread[:, :], ps_ot, group_var)
                if conv:
                    wait(pe, chain, i, MIX * LEVELS)
                    for m in range(CT):
                        product("cv", CT + m, keep["cv1"][:, :, cols(m)], cat1, cv)
                if attn:
                    wait(pe, f_split, i - 1, 2 * CT)
                    for m in range(CT):
                        slot = claim("qv", m)
                        for h in range(2):
                            hs = slice(h * HALF, (h + 1) * HALF)
                            last = split_product(slot[:, hs], [(keep["w1_hi"][:, k, cols(m)], keep["w1_lo"][:, k, cols(m)],
                                                                f_hi[:, k, hs], f_lo[:, k, hs]) for k in range(CT)])
                        last.then_inc(qv.sem, 1)
                    for half in range(2):
                        slot = claim("qv", 2 + half)
                        for m in range(4):
                            px = cols(4 * half + m)
                            last = split_product(slot[:, m * C:(m + 1) * C], [(f_hi[:, k, px], f_lo[:, k, px], keep["w2_hi"][:, k],
                                                                              keep["w2_lo"][:, k]) for k in range(CT)])
                        last.then_inc(qv.sem, 1)
                    score(0)
                    for t in range(TILES):
                        if t + 1 < TILES:
                            score(t + 1)
                        if t:
                            mix(t - 1)
                        turn(t)
                        if t > 1:
                            turn_back(t - 2)
                    mix(TILES - 1)
                    turn_back(TILES - 2)
                    turn_back(TILES - 1)
                if conv:
                    wait(pe, taps, i, 2 * KT * STAGES)
                    for m in range(KT):
                        product("c1", m, keep["c1"][:, :, cols(m)], flat(a), c1)
                    wait(pe, gated, i, KT)
                    for m in range(CT):
                        product("ce", m, keep["cvend"][:, :, cols(m)], flat(y), cvend)

            steps(pe, step)

        @block.scalar
        def _(act):
            def pad_first(i):
                wait(act, chain_loaded, i, 16)
                nc.scalar.copy(inner(0), image2d(chain_in[:, :])).then_inc(padded.sem, 1)
                nc.scalar.copy(zero[:, :, 2:2 + W], image2d(chain_in[:, :])).then_inc(padded.sem, 1)

            def pad_next(i, level):
                wait(act, chain, i, MIX * level)
                nc.scalar.copy(zero[:, :, 2:2 + W], inner(level)).then_inc(padded.sem, 1)

            def average(i, level):
                wait(act, summed, i, 6 * (level + 1))
                nc.scalar.mul(sum_b[:, :, :], sum_b[:, :, :], (1.0 - T_POOL) / K2).then_inc(averaged.sem, 1)

            def step(i, conv, attn, chained):
                def silu_cv(k):
                    c = ORDER[k]
                    wait(act, cv, i, k + 1)
                    bias = keep["b_cv1"][:, c:c + 1] if c < CT else keep["b_cv2"][:, c - CT:c - CT + 1]
                    nc.scalar.activation(y[:, c], slots_of["cv", k][:, :], ACT.Silu, bias=bias).then_inc(y_ready.sem, 1)

                def centre_tap(n):
                    c, s, src, dst = stage(n)
                    if n:
                        wait(act, taps, i, 2 * n)
                    else:
                        wait(act, chain, i, MIX * LEVELS)
                    if s == 0:
                        wait(act, y_ready, i, n // STAGES + 1)
                    if attn and n == 11:
                        wait(act, f_split, i - 1, 2 * CT)
                    nc.scalar.activation(dst, src, ACT.Identity, scale=keep["taps"][:, s, c, 1:2],
                                         bias=keep["b_taps"][:, s, c:c + 1]).then_inc(centre.sem, 1)

                def exponent(t):
                    wait(act, maxed, i - 1, t + 1)
                    if t:
                        wait(act, turned, i - 1, t)
                    nc.scalar.activation(prob[:, :], slots_of["s", t][:, :], ACT.Exp, bias=minus_max[:, t:t + 1],
                                         accum_out=row_sum[:, t:t + 1]).then_inc(prob_done.sem, 1)

                def turned_hi(t):
                    wait(act, turned, i - 1, t + 1)
                    nc.scalar.copy(pt_hi[:, t % 2], slots_of["t", t][:, :]).then_inc(pt_hi_done.sem, 1)

                def scale_mixed(t):
                    wait(act, pv, i - 1, t + 1)
                    wait(act, inverse, i - 1, t + 1)
                    nc.scalar.activation(mixed[:, t % 2], ps_o[:, 0:C], ACT.Copy, scale=row_inv[:, t:t + 1]).then_inc(mixed_done.sem, 1)

                before = iter(range(BEFORE if attn else KT * STAGES))
                slots_of = slot_plan(conv, attn)
                if conv:
                    silu_cv(0)
                    centre_tap(next(before))
                    silu_cv(1)
                    centre_tap(next(before))
                if attn:
                    for t in range(CT):
                        wait(act, norm, i - 1, 6)
                        nc.scalar.activation(a[:, t], x1[:, t], ACT.Identity, scale=rstd[:, t:t + 1],
                                             bias=shift[:, t:t + 1]).then_inc(f_done.sem, 1)
                if conv:
                    centre_tap(next(before))
                    silu_cv(2)
                    centre_tap(next(before))
                    silu_cv(3)
                    for n in before:
                        centre_tap(n)
                if attn:
                    for k in range(4):
                        wait(act, qv, i - 1, k + 1)
                        src = slots_of["qv", k][:, :]
                        if k < 2:
                            nc.scalar.activation(q_hi[:, k], src, ACT.Copy, scale=C ** -0.5).then_inc(qv_hi.sem, 1)
                        else:
                            nc.scalar.copy(v_hi[:, 4 * (k - 2):4 * (k - 1)].rearrange("p m c -> p (m c)"), src).then_inc(qv_hi.sem, 1)
                if chained:
                    wait(act, cv, i, 2 * CT)
                    pad_first(i + 1)
                if attn:
                    exponent(0)
                    for t in range(TILES):
                        now = iter(stages_of(t) if conv else ())
                        for n in now:
                            centre_tap(n)
                            break
                        if t:
                            turned_hi(t - 1)
                        for n in now:
                            centre_tap(n)
                        if t > 1:
                            scale_mixed(t - 2)
                        if t + 1 < TILES:
                            exponent(t + 1)
                    turned_hi(TILES - 1)
                    scale_mixed(TILES - 2)
                    scale_mixed(TILES - 1)
                if chained:
                    average(i + 1, 0)
                    pad_next(i + 1, 1)
                    average(i + 1, 1)
                    pad_next(i + 1, 2)
                if conv:
                    for m in range(CT):
                        if m == 1 and chained:
                            average(i + 1, 2)
                        wait(act, cvend, i, m + 1)
                        nc.scalar.activation(a[:, m], slots_of["ce", m][:, :], ACT.Silu, bias=keep["b_cvend"][:, m:m + 1]).then_inc(ended.sem, 1)

            act.wait_ge(ready.sem, 2 + 7)
            pad_first(0)
            for level in range(LEVELS):
                average(0, level)
                if level + 1 < LEVELS:
                    pad_next(0, level + 1)
            steps(act, step)

        @block.vector
        def _(dve):
            for k in range(LEVELS + 1):
                if k < LEVELS:
                    nc.vector.memset(wide[:, k, :, 0:2], LOWEST).then_inc(ready.sem, 1)
                    nc.vector.memset(wide[:, k, :, 2 + W:WP], LOWEST).then_inc(ready.sem, 1)
            nc.vector.memset(tall[:, :, :], LOWEST).then_inc(ready.sem, 1)
            dve.wait_ge(ready.sem, 2 + 7)
            mh = work[:, 0].rearrange("p (h w) -> p h w", w=WP - 2)
            mv2 = work[:, 0].rearrange("p (h w) -> p h w", w=W)
            m4 = image2d(work[:, 1, 0:N])

            def maxima(own, level, i):
                if level == 0:
                    wait(dve, padded, i, 1)
                src = wide[:, level]

                def larger(out, in0, in1):
                    own.did(nc.vector.tensor_tensor(out, in0, in1, ALU.max))
                    own.wait()

                larger(mh, src[:, :, 0:WP - 2], src[:, :, 1:WP - 1])
                larger(m4, mh[:, :, 0:W], mh[:, :, 2:W + 2])
                larger(tall[:, 2:H + 2], m4, src[:, :, 4:WP])
                larger(mv2, tall[:, 0:H + 2], tall[:, 1:H + 3])
                larger(m4, mv2[:, 0:H], mv2[:, 2:H + 2])
                larger(m4, m4, tall[:, 4:H + 4])

            def mixture(own, level, i):
                wait(dve, averaged, i, level + 1)
                own.did(nc.vector.scalar_tensor_tensor(inner(level + 1), m4, T_POOL, sum_b[:, :, :], ALU.mult, ALU.add))
                own.wait()

            def step(i, conv, attn, chained):
                def outer_taps(n):
                    c, s, src, dst = stage(n)
                    wait(dve, centre, i, n + 1)
                    src, dst = image2d(src), image2d(dst)
                    d = 1 if s < 2 else 2
                    for k, tap in ((0, 0), (1, 2)):
                        if tap == 0:
                            far, near = slice(d, W), slice(0, W - d)
                        else:
                            far, near = slice(0, W - d), slice(d, W)
                        o, u = (dst[:, :, far], src[:, :, near]) if s % 2 == 0 else (dst[:, far], src[:, near])
                        if k:
                            wait(dve, taps, i, 2 * n + 1)
                        nc.vector.scalar_tensor_tensor(o, u, keep["taps"][:, s, c, tap:tap + 1], o, ALU.mult, ALU.add).then_inc(taps.sem, 1)

                def turned_lo(t):
                    wait(dve, pt_hi_done, i - 1, t + 1)
                    nc.vector.tensor_tensor(pt_lo[:, t % 2], slots_of["t", t][:, :], pt_hi[:, t % 2].bitcast(F32),
                                            ALU.subtract).then_inc(pt_lo_done.sem, 1)

                def maximum(t):
                    wait(dve, scores, i - 1, t + 1)
                    nc.vector.tensor_reduce(minus_max[:, t:t + 1], slots_of["s", t][:, :], AX, ALU.max, negate=True).then_inc(maxed.sem, 1)

                def invert(t):
                    wait(dve, prob_done, i - 1, t + 1)
                    nc.vector.reciprocal(row_inv[:, t:t + 1], row_sum[:, t:t + 1]).then_inc(inverse.sem, 1)

                def add_attention(t):
                    wait(dve, back, i - 1, t + 1)
                    part = x1[:, :, t * P:(t + 1) * P]
                    nc.vector.tensor_tensor(part, ps_ot[:, 0:C].rearrange("p (d n) -> p d n", d=CT), part, ALU.add).then_inc(result.sem, 1)

                def gate(m):
                    wait(dve, c1, i, m + 1)
                    nc.vector.scalar_tensor_tensor(y[:, m], slots_of["c1", m][:, :], keep["b_c1"][:, m:m + 1], y[:, m],
                                                   ALU.add, ALU.mult).then_inc(gated.sem, 1)

                def add_l0(m):
                    wait(dve, x_loaded, i, 16)
                    wait(dve, ended, i, m + 1)
                    nc.vector.tensor_tensor(x1[:, m], a[:, m], x1[:, m], ALU.add).then_inc(added.sem, 1)
                    wait(dve, added, i, m + 1)
                    for h in range(2):
                        nc.vector.bn_stats(stats[:, m, h, :], x1[:, m, h * HALF:(h + 1) * HALF]).then_inc(bn.sem, 1)

                slots_of = slot_plan(conv, attn)
                before = iter(range(BEFORE if attn else KT * STAGES))
                if attn:
                    small = Steps(dve, norm, i - 1)
                    wait(dve, group_mean, i - 1, 1)
                    small.did(nc.vector.tensor_tensor(dev[:, :], mv[:, :, 0], ps_o[:, 0:CT], ALU.subtract))
                    small.wait()
                    small.did(nc.vector.tensor_tensor(dev[:, :], dev[:, :], dev[:, :], ALU.mult))
                    small.wait()
                    small.did(nc.vector.tensor_tensor(spread[:, :], dev[:, :], mv[:, :, 1], ALU.add))
                if conv:
                    outer_taps(next(before))
                    outer_taps(next(before))
                if attn:
                    wait(dve, group_var, i - 1, 1)
                    small.did(nc.vector.tensor_scalar(spread[:, :], ps_ot[:, 0:CT], 1e-5, None, ALU.add))
                    small.did(nc.vector.tensor_scalar(gmean[:, :], ps_o[:, 0:CT], -1.0, None, ALU.mult))
                    small.wait()
                    wait(dve, rstd_done, i - 1, 1)
                    small.did(nc.vector.tensor_tensor(shift[:, :], gmean[:, :], rstd[:, :], ALU.mult))
                if conv:
                    outer_taps(next(before))
                if attn:
                    for t in range(CT):
                        wait(dve, f_done, i - 1, t + 1)
                        nc.vector.tensor_copy(f_hi[:, t], a[:, t]).then_inc(f_split.sem, 1)
                        wait(dve, f_split, i - 1, 2 * t + 1)
                        nc.vector.tensor_tensor(f_lo[:, t], a[:, t], f_hi[:, t].bitcast(F32), ALU.subtract).then_inc(f_split.sem, 1)
                if conv:
                    for n in before:
                        outer_taps(n)
                if attn:
                    for k in range(4):
                        wait(dve, qv_hi, i - 1, k + 1)
                        src = slots_of["qv", k][:, :]
                        if k < 2:
                            nc.vector.scalar_tensor_tensor(q_lo[:, k], src, C ** -0.5, q_hi[:, k].bitcast(F32),
                                                           ALU.mult, ALU.subtract).then_inc(qv_lo.sem, 1)
                        else:
                            m = slice(4 * (k - 2), 4 * (k - 1))
                            nc.vector.tensor_tensor(v_lo[:, m].rearrange("p m c -> p (m c)"), src,
                                                    v_hi[:, m].rearrange("p m c -> p (m c)").bitcast(F32), ALU.subtract).then_inc(qv_lo.sem, 1)
                    maximum(0)
                    for t in range(TILES):
                        if t:
                            turned_lo(t - 1)
                        now = iter(stages_of(t) if conv else ())
                        for n in now:
                            outer_taps(n)
                            break
                        if t + 1 < TILES:
                            maximum(t + 1)
                        for n in now:
                            outer_taps(n)
                        invert(t)
                        if t > 1:
                            add_attention(t - 2)
                    turned_lo(TILES - 1)
                    add_attention(TILES - 2)
                    add_attention(TILES - 1)
                if chained:
                    own = Steps(dve, chain, i + 1)
                    wait(dve, taps, i, 2 * KT * STAGES)
                    maxima(own, 0, i + 1)
                    mixture(own, 0, i + 1)
                if conv:
                    gate(0)
                if chained:
                    maxima(own, 1, i + 1)
                if conv:
                    gate(1)
                    gate(2)
                if chained:
                    mixture(own, 1, i + 1)
                if conv:
                    gate(3)
                if chained:
                    maxima(own, 2, i + 1)
                if conv:
                    add_l0(0)
                if chained:
                    mixture(own, 2, i + 1)
                if conv:
                    add_l0(1)
                    wait(dve, bn, i, 4)
                    dve.sem_inc(stats_gate, 1)
                    for m in range(CT):
                        nc.vector.bn_aggr(mv[:, m, :], stats[:, m].rearrange("p h s -> p (h s)")).then_inc(bn.sem, 1)

            own = Steps(dve, chain, 0)
            for level in range(LEVELS):
                maxima(own, level, 0)
                mixture(own, level, 0)
            steps(dve, step)


def program(nc, x, w, consts, levels, out):
    with ExitStack() as ctx:
        keep = kept_tensors(ctx, nc)
        rmc = ctx.enter_context(nc.sbuf_tensor("rmc", [P, B], F32))
        phase_a(nc, x, w, consts, keep, levels, rmc)
        phase_b(nc, consts, keep, levels, rmc)
        phase_c(nc, x, out, keep, levels)


def kernel(**inputs):
    import numpy as np
    import concourse.bacc as bacc
    from concourse.bass_utils import run_bass_kernel_spmd

    nc = bacc.Bacc("TRN2", target_bir_lowering=False, num_devices=1)
    arrays = {"x": np.ascontiguousarray(inputs["x"]), "columns": columns(inputs)}
    for k in ("sta", "cv1", "cv2", "cvend", "c1"):
        arrays["w_" + k] = np.ascontiguousarray(inputs["L0_conv_w_" + k][:, :, 0, 0].T)
    for k in ("w1", "w2"):
        arrays["w_" + k] = np.ascontiguousarray(inputs["L1_conv_" + k].T)
    for k, v in constants().items():
        arrays["const_" + k] = v
    aps = {k: nc.dram_tensor("in_" + k, v.shape, F32, kind="ExternalInput").ap() for k, v in arrays.items()}
    levels = nc.dram_tensor("levels", ((LEVELS + 1) * B, P, N), F32, kind="Internal").ap()
    out = nc.dram_tensor("out", (B, C, H, W), F32, kind="ExternalOutput").ap()
    w = {k[2:]: v for k, v in aps.items() if k.startswith("w_")}
    w["columns"] = aps["columns"]
    consts = {k[6:]: v for k, v in aps.items() if k.startswith("const_")}
    program(nc, aps["x"], w, consts, levels, out)
    r = run_bass_kernel_spmd(nc, [{"in_" + k: v for k, v in arrays.items()}], core_ids=[0])
    return r.results[0]["out"]
```

```python
import concourse.bass as bass
from concourse import mybir
from contextlib import ExitStack

F32 = mybir.dt.float32
F32R = mybir.dt.float32r
ALU = mybir.AluOpType
ACT = mybir.ActivationFunctionType
AX = mybir.AxisListType.X
RMAX = bass.bass_isa.ReduceOp.max

P = 128
B = 8
C = 256
CT = C // P
H = W = 32
N = H * W
HALF = 512
C4 = 512
KT = C4 // P
LEVELS = 3
WP = W + 4
GROUP = C // 32
T_POOL = 0.9
K2 = 25
LOWEST = -3.4028235e38
STAGES = 4
COLUMNS = {"b_sta": 1, "b_cv1": CT, "b_cv2": CT, "b_cvend": CT, "b_c1": KT,
           "taps": STAGES * KT * 3, "b_taps": STAGES * KT}
EXP_LN = "natural_log_exp_and_others"


class Signal:

    def __init__(self, sem, per):
        self.sem, self.per = sem, per

    def at(self, image, k):
        return image * self.per + k


class Steps:

    def __init__(self, eng, counted, image, k=0):
        self.eng, self.counted, self.image, self.k = eng, counted, image, k

    def did(self, ins):
        self.k += 1
        ins.then_inc(self.counted.sem, 1)

    def wait(self):
        self.eng.wait_ge(self.counted.sem, self.counted.at(self.image, self.k))


MIX = 7


def wait(eng, sig, image, k):
    eng.wait_ge(sig.sem, sig.at(image, k))


def image2d(ap):
    return ap.rearrange("p (h w) -> p h w", w=W)


class Chain:

    def __init__(self, ctx, nc):
        def sb(name, shape):
            return ctx.enter_context(nc.sbuf_tensor(name, shape, F32))

        def counted(name, per):
            return Signal(ctx.enter_context(nc.semaphore("chain_" + name)), per)

        self.nc = nc
        self.stem = sb("chain_in", [P, N])
        self.wide = sb("wide", [P, LEVELS + 1, H, WP])
        self.zero = sb("zero", [P, H, WP])
        self.tall = sb("tall", [P, H + 4, W])
        self.tall_sum = sb("tall_sum", [P, H + 4, W])
        self.sum_a = sb("sum_a", [P, (H + 2) * W])
        self.sum_b = sb("sum_b", [P, H, W])
        self.work = sb("work", [P, 2, (H + 2) * W])
        self.loaded = counted("loaded", 16)
        self.padded = counted("padded", 1 + LEVELS)
        self.done = counted("done", MIX * LEVELS)
        self.summed = counted("summed", 6 * LEVELS)
        self.averaged = counted("averaged", LEVELS)
        self.borders = ctx.enter_context(nc.semaphore("chain_borders"))
        self.gate = ctx.enter_context(nc.semaphore("chain_gate"))
        self.n_borders = 2 + 2 * LEVELS + 1

    def inner(self, k):
        return self.wide[:, k, :, 2:2 + W]

    def set_sum_borders(self):
        self.nc.gpsimd.memset(self.zero[:, :, :], 0.0).then_inc(self.borders, 1)
        self.nc.gpsimd.memset(self.tall_sum[:, :, :], 0.0).then_inc(self.borders, 1)

    def set_max_borders(self):
        for k in range(LEVELS):
            self.nc.vector.memset(self.wide[:, k, :, 0:2], LOWEST).then_inc(self.borders, 1)
            self.nc.vector.memset(self.wide[:, k, :, 2 + W:WP], LOWEST).then_inc(self.borders, 1)
        self.nc.vector.memset(self.tall[:, :, :], LOWEST).then_inc(self.borders, 1)

    def pad_first(self, act, i):
        wait(act, self.loaded, i, 16)
        self.nc.scalar.copy(self.inner(0), image2d(self.stem[:, :])).then_inc(self.padded.sem, 1)
        self.nc.scalar.copy(self.zero[:, :, 2:2 + W], image2d(self.stem[:, :])).then_inc(self.padded.sem, 1)

    def pad_next(self, act, i, level):
        wait(act, self.done, i, MIX * level)
        act.sem_inc(self.gate, 1)
        self.nc.scalar.copy(self.zero[:, :, 2:2 + W], self.inner(level)).then_inc(self.padded.sem, 1)

    def average(self, act, i, level):
        wait(act, self.summed, i, 6 * (level + 1))
        self.nc.scalar.mul(self.sum_b[:, :, :], self.sum_b[:, :, :], (1.0 - T_POOL) / K2).then_inc(self.averaged.sem, 1)

    def box_sums_start(self, pool, i, level):
        wait(pool, self.padded, i, 2 + level)
        own = Steps(pool, self.summed, i, 6 * level)
        sa = self.sum_a[:, :].rearrange("p (h w) -> p h w", w=WP - 2)
        self.add(own, sa, self.zero[:, :, 0:WP - 2], self.zero[:, :, 1:WP - 1], first=True)
        self.add(own, self.sum_b[:, :, :], sa[:, :, 0:W], sa[:, :, 2:W + 2])
        self.add(own, self.tall_sum[:, 2:H + 2], self.sum_b[:, :, :], self.zero[:, :, 4:WP])
        self.add(own, self.sum_rows(), self.tall_sum[:, 0:H + 2], self.tall_sum[:, 1:H + 3])

    def box_sums_end(self, pool, i, level):
        own = Steps(pool, self.summed, i, 6 * level + 4)
        sv = self.sum_rows()
        self.add(own, self.sum_b[:, :, :], sv[:, 0:H], sv[:, 2:H + 2])
        self.add(own, self.sum_b[:, :, :], self.sum_b[:, :, :], self.tall_sum[:, 4:H + 4])

    def add(self, own, out, in0, in1, first=False):
        if not first:
            own.wait()
        own.did(self.nc.gpsimd.tensor_tensor(out, in0, in1, ALU.add))

    def sum_rows(self):
        return self.sum_a[:, :].rearrange("p (h w) -> p h w", w=W)

    def maxima(self, dve, i, level):
        wait(dve, self.padded, i, 1)
        own = Steps(dve, self.done, i, MIX * level)
        mh = self.work[:, 0].rearrange("p (h w) -> p h w", w=WP - 2)
        mv = self.work[:, 0].rearrange("p (h w) -> p h w", w=W)
        m4 = image2d(self.work[:, 1, 0:N])
        src = self.wide[:, level]

        def larger(out, in0, in1):
            own.did(self.nc.vector.tensor_tensor(out, in0, in1, ALU.max))
            own.wait()

        larger(mh, src[:, :, 0:WP - 2], src[:, :, 1:WP - 1])
        larger(m4, mh[:, :, 0:W], mh[:, :, 2:W + 2])
        larger(self.tall[:, 2:H + 2], m4, src[:, :, 4:WP])
        larger(mv, self.tall[:, 0:H + 2], self.tall[:, 1:H + 3])
        larger(m4, mv[:, 0:H], mv[:, 2:H + 2])
        larger(m4, m4, self.tall[:, 4:H + 4])

    def mixture(self, dve, i, level):
        wait(dve, self.averaged, i, level + 1)
        own = Steps(dve, self.done, i, MIX * level + 6)
        own.did(self.nc.vector.scalar_tensor_tensor(self.inner(level + 1), image2d(self.work[:, 1, 0:N]), T_POOL,
                                                    self.sum_b[:, :, :], ALU.mult, ALU.add))
        own.wait()



def phase_a(nc, x, w, consts, keep, levels, rmc):
    with ExitStack() as ctx:
        def sb(name, shape, dt=F32):
            return ctx.enter_context(nc.sbuf_tensor(name, shape, dt))

        def sem(name):
            return ctx.enter_context(nc.semaphore(name))

        x_all = sb("x_all", [P, B, CT, N])
        xn = sb("xn", [P, 2, CT, N])
        stem = sb("stem", [P, 2, N])
        w_sta = sb("w_sta", [P, CT, P])
        w_attn = sb("w_attn", [P, 2, CT, C])
        stats = sb("stats", [P, B, CT, 2, 6])
        mv = sb("mv", [P, B * CT, 2])
        dev = sb("dev", [P, B * CT])
        spread = sb("spread", [P, B * CT])
        rstd = sb("rstd", [P, B * CT])
        shift = sb("shift", [P, B * CT])
        ps = ctx.enter_context(nc.psum_tensor("ps_a", [P, 2, N], F32))
        ps_mean = ctx.enter_context(nc.psum_tensor("ps_mean", [P, HALF], F32))
        ps_var = ctx.enter_context(nc.psum_tensor("ps_var", [P, HALF], F32))

        x_in = [sem(f"a_x_in{i}") for i in range(B)]
        weights_in = sem("a_weights_in")
        stats_done = sem("a_stats_done")
        mv_done = sem("a_mv_done")
        mean_done = sem("a_mean_done")
        dev_done = sem("a_dev_done")
        var_done = sem("a_var_done")
        eps_done = sem("a_eps_done")
        rstd_done = sem("a_rstd_done")
        shift_done = sem("a_shift_done")
        split_done = sem("a_split_done")
        xn_done = sem("a_xn_done")
        sta_done = sem("a_sta_done")
        stem_done = sem("a_stem_done")
        max_done = sem("a_max_done")
        stored = [sem(f"a_stored{u}") for u in range(2)]
        block = ctx.enter_context(nc.Block())

        x_v = x.rearrange("b (t p) h w -> b p t (h w)", p=P)

        @block.sync
        def _(sp):
            for i in range(B):
                sp.dma_start(x_all[:, i], x_v[i]).then_inc(x_in[i], 16)
            for u in range(2):
                sp.sem_inc(stored[u], 16)
            with sp.Fori(0, B // 2) as pair:
                for u in range(2):
                    n = pair * 2 + u
                    sp.wait_ge(stem_done, n + 3)
                    sp.dma_start(levels[n], stem[:, u]).then_inc(stored[u], 16)
            for u in range(2):
                sp.wait_ge(stored[u], 16 * (B // 2 + 1))

        @block.scalar
        def _(act):
            loads = [(keep[k][:, :], consts[k]) for k in ("ident", "group")]
            loads += [(w_sta[:, :, :], w["sta"].rearrange("(t p) o -> p t o", p=P)),
                      (w_attn[:, 0], w["w1"].rearrange("(t p) o -> p t o", p=P)),
                      (w_attn[:, 1], w["w2"].rearrange("(t p) o -> p t o", p=P))]
            loads += [(keep[k][:, :, :], w[k].rearrange("(t p) o -> p t o", p=P)) for k in ("cv1", "cv2", "cvend", "c1")]
            loads.append((keep["columns"][:, :], w["columns"]))
            for dst, src in loads:
                act.dma_start(dst, src).then_inc(weights_in, 16)
            act.wait_ge(weights_in, 16 * len(loads))
            act.sem_inc(stem_done, 2)
            with act.Fori(0, B // 2) as pair:
                for u in range(2):
                    n = pair * 2 + u
                    act.wait_ge(sta_done, n + 3)
                    act.wait_ge(max_done, n + 1)
                    act.wait_ge(stored[u], 16 * pair + 16)
                    nc.scalar.activation(stem[:, u], ps[:, u], ACT.Silu, bias=keep["b_sta"]).then_inc(stem_done, 1)

        @block.tensor
        def _(pe):
            pe.sem_inc(sta_done, 2)
            pe.wait_ge(stem_done, 2)
            pe.wait_ge(mv_done, B * CT)
            nc.tensor.matmul(ps_mean[:, 0:B * CT], keep["group"][:, :], mv[:, :, 0], start=True, stop=True).then_inc(mean_done, 1)
            pe.wait_ge(dev_done, 3)
            nc.tensor.matmul(ps_var[:, 0:B * CT], keep["group"][:, :], spread[:, :], start=True, stop=True).then_inc(var_done, 1)
            with pe.Fori(0, B // 2) as pair:
                for u in range(2):
                    n = pair * 2 + u
                    pe.wait_ge(xn_done, CT * n + CT)
                    pe.wait_ge(stem_done, n + 1)
                    for h in range(2):
                        for k in range(CT):
                            last = nc.tensor.matmul(ps[:, u, h * HALF:(h + 1) * HALF], w_sta[:, k, :],
                                                    xn[:, u, k, h * HALF:(h + 1) * HALF], start=(k == 0), stop=(k == CT - 1))
                    last.then_inc(sta_done, 1)

        @block.gpsimd
        def _(pool):
            nc.gpsimd.memset(keep["minus_half"][:, :], -0.5).then_inc(rstd_done, 1)
            pool.wait_ge(rstd_done, 1)
            pool.wait_ge(eps_done, 1)
            nc.gpsimd.tensor_tensor(rstd[:, :], spread[:, :], keep["minus_half"][:, :], ALU.pow).then_inc(rstd_done, 1)

        @block.vector
        def _(dve):
            for i in range(B):
                dve.wait_ge(x_in[i], 16)
                for t in range(CT):
                    for h in range(2):
                        nc.vector.bn_stats(stats[:, i, t, h, :], x_all[:, i, t, h * HALF:(h + 1) * HALF]).then_inc(stats_done, 1)
            dve.wait_ge(stats_done, B * CT * 2)
            for i in range(B):
                for t in range(CT):
                    nc.vector.bn_aggr(mv[:, i * CT + t, :], stats[:, i, t].rearrange("p h s -> p (h s)")).then_inc(mv_done, 1)
            dve.wait_ge(mean_done, 1)
            dve.wait_ge(mv_done, B * CT)
            nc.vector.tensor_tensor(dev[:, :], mv[:, :, 0], ps_mean[:, 0:B * CT], ALU.subtract).then_inc(dev_done, 1)
            dve.wait_ge(dev_done, 1)
            nc.vector.tensor_tensor(dev[:, :], dev[:, :], dev[:, :], ALU.mult).then_inc(dev_done, 1)
            dve.wait_ge(dev_done, 2)
            nc.vector.tensor_tensor(spread[:, :], dev[:, :], mv[:, :, 1], ALU.add).then_inc(dev_done, 1)
            dve.wait_ge(stem_done, 2)
            for n, name in enumerate(("w1", "w2")):
                nc.vector.tensor_copy(keep[name + "_hi"][:, :, :], w_attn[:, n]).then_inc(split_done, 1)
                dve.wait_ge(split_done, 2 * n + 1)
                nc.vector.tensor_tensor(keep[name + "_lo"][:, :, :], w_attn[:, n], keep[name + "_hi"][:, :, :].bitcast(F32),
                                        ALU.subtract).then_inc(split_done, 1)
            dve.wait_ge(var_done, 1)
            nc.vector.tensor_scalar(spread[:, :], ps_var[:, 0:B * CT], 1e-5, None, ALU.add).then_inc(eps_done, 1)
            dve.wait_ge(rstd_done, 2)
            nc.vector.scalar_tensor_tensor(shift[:, :], ps_mean[:, 0:B * CT], -1.0, rstd[:, :], ALU.mult, ALU.mult).then_inc(shift_done, 1)
            dve.wait_ge(shift_done, 1)
            dve.sem_inc(max_done, 2)

            def normalise(n, u):
                dve.wait_ge(sta_done, n + 1)
                for t in range(CT):
                    nc.vector.tensor_scalar(xn[:, u, t], x_all[:, n, t], rstd[:, bass.ds(n * CT + t, 1)],
                                            shift[:, bass.ds(n * CT + t, 1)], ALU.mult, ALU.add).then_inc(xn_done, 1)

            def maximum(n, u):
                dve.wait_ge(stem_done, n + 3)
                nc.vector.reduce_max(rmc[:, bass.ds(n, 1)], stem[:, u], AX).then_inc(max_done, 1)

            normalise(0, 0)
            normalise(1, 1)
            with dve.Fori(0, B // 2 - 1) as pair:
                for u in range(2):
                    normalise(pair * 2 + u + 2, u)
                    maximum(pair * 2 + u, u)
            maximum(B - 2, 0)
            maximum(B - 1, 1)


def phase_b(nc, consts, keep, levels, rmc, chain):
    with ExitStack() as ctx:
        def sb(name, shape, dt=F32):
            return ctx.enter_context(nc.sbuf_tensor(name, shape, dt))

        def sem(name):
            return ctx.enter_context(nc.semaphore("b_" + name))

        box_raw = sb("box_raw", [P, 8 * W])
        box = sb("box", [P, 8 * W], F32R)
        y_in = sb("y_in", [P, 2, N])
        e = sb("e", [P, 2, N])
        ey = sb("ey", [P, 2, N])
        e_hi = sb("e_hi", [P, 2, N], F32R)
        e_lo = sb("e_lo", [P, 2, N], F32R)
        ey_hi = sb("ey_hi", [P, 2, N], F32R)
        ey_lo = sb("ey_lo", [P, 2, N], F32R)
        r = sb("r", [P, 2, N])
        newton = sb("newton", [P, 2, N])
        y_out = sb("y_out", [P, 2, N])
        tile_max = sb("tile_max", [P, 1])
        batch_max = sb("batch_max", [P, 1])
        minus_max = sb("minus_max", [P, 1])
        eps = sb("eps", [P, 1])
        ps_t = ctx.enter_context(nc.psum_tensor("ps_t", [P, 2, N], F32))
        ps_e = ctx.enter_context(nc.psum_tensor("ps_e", [P, N], F32))
        ps_ey = ctx.enter_context(nc.psum_tensor("ps_ey", [P, N], F32))

        box_in, box_ready = sem("box_in"), sem("box_ready")
        loaded = [sem(f"loaded{u}") for u in range(2)]
        turned = sem("turned")
        exp_done, e_hi_done, e_lo_done = sem("exp_done"), sem("e_hi_done"), sem("e_lo_done")
        ey_done, ey_hi_done, ey_lo_done = sem("ey_done"), sem("ey_hi_done"), sem("ey_lo_done")
        sum_e_done, sum_ey_done = sem("sum_e_done"), sem("sum_ey_done")
        r_done, newton_done, y_done = sem("r_done"), sem("newton_done"), sem("y_done")
        col_max_done, tile_max_done = sem("col_max_done"), sem("tile_max_done")
        batch_max_done, minus_max_done = sem("batch_max_done"), sem("minus_max_done")
        eps_set, gate = sem("eps_set"), sem("gate")
        stored = [sem(f"stored{u}") for u in range(2)]
        block = ctx.enter_context(nc.Block())

        def images(eng, head, step, tail, unroll_final=False):
            def level_of(level, final):
                def one(h, u, m=None):
                    step(level, level * (B // 2) + h, h, u, m, behind=m != 0, ahead=2 if m is None else min(2, B - 1 - m), final=final)

                head(level, final)
                if final and unroll_final:
                    for m in range(B):
                        one(m // 2, m % 2, m)
                else:
                    one(0, 0, 0)
                    with eng.Fori(0, B // 2 - 2) as h:
                        one(h, 1)
                        one(h + 1, 0)
                    for m in range(B - 3, B):
                        one(m // 2, m % 2, m)
                tail(level, level * (B // 2) + B // 2, final)

            with eng.Fori(0, LEVELS - 1) as level:
                level_of(level, False)
            level_of(LEVELS - 1, True)

        @block.sync
        def _(sp):
            def load(q, u):
                n = q * 2 + u
                sp.wait_ge(turned, n + 1)
                sp.wait_ge(stored[u], q * 16 + 16)
                sp.dma_start(y_in[:, u], levels[n]).then_inc(loaded[u], 16)

            def store(q, u):
                n = q * 2 + u
                sp.wait_ge(y_done, n + 3)
                sp.dma_start(levels[n + B], y_out[:, u]).then_inc(stored[u], 16)

            def head(level, final):
                for u in range(2):
                    load(level * (B // 2) + 1, u)

            def step(level, q, h, u, m, behind, ahead, final):
                if m is None or m < (B - 4 if final else B - 2):
                    load(q + 2, u)
                if behind:
                    store(q - 1 + u, 1 - u)

            sp.dma_start(chain.stem[:, :], levels[0]).then_inc(chain.loaded.sem, 16)
            sp.dma_start(box_raw[:, :], consts["box"]).then_inc(box_in, 16)
            for u in range(2):
                sp.sem_inc(stored[u], 16 * (B // 2))
            for u in range(2):
                load(0, u)
            images(sp, head, step, lambda level, q, final: store(q - 1, 1), unroll_final=True)
            for u in range(2):
                sp.wait_ge(stored[u], 16 * (B // 2) * (LEVELS + 1))

        @block.tensor
        def _(pe):
            def turn(q, u):
                n = q * 2 + u
                pe.wait_ge(loaded[u], q * 16 + 16)
                pe.wait_ge(ey_done, n + 1)
                for k in range(N // P):
                    last = nc.tensor.transpose(ps_t[:, u, k * P:(k + 1) * P], y_in[:, u, k * P:(k + 1) * P], keep["ident"][:, :])
                last.then_inc(turned, 1)

            def box_sum(out, hi, lo):
                rows, bank = P // W, HALF // W
                started = set()
                for k in range(N // P):
                    first, end = max(rows * k - 2, 0), min(rows * k + rows + 2, H)
                    for b in range(first // bank, (end - 1) // bank + 1):
                        r0, r1 = max(first, b * bank), min(end, (b + 1) * bank)
                        c0 = (r0 - (rows * k - 2)) * W
                        for part in (hi, lo):
                            last = nc.tensor.matmul(out[:, r0 * W:r1 * W], part[:, k * P:(k + 1) * P],
                                                    box[:, c0:c0 + (r1 - r0) * W], start=(b not in started),
                                                    stop=(k == N // P - 1), skip_group_check=True)
                            started.add(b)
                return last

            def sum_e(q, u):
                n = q * 2 + u
                pe.wait_ge(e_hi_done, n + 1)
                pe.wait_ge(e_lo_done, n + 1)
                pe.wait_ge(newton_done, n * 2 + 1)
                box_sum(ps_e, e_hi[:, u], e_lo[:, u]).then_inc(sum_e_done, 1)

            def sum_ey(q, u):
                n = q * 2 + u
                pe.wait_ge(ey_hi_done, n + 1)
                pe.wait_ge(ey_lo_done, n + 3)
                pe.wait_ge(y_done, n + 2)
                box_sum(ps_ey, ey_hi[:, u], ey_lo[:, u]).then_inc(sum_ey_done, 1)

            def head(level, final):
                for u in range(2):
                    turn(level * (B // 2), u)

            def step(level, q, h, u, m, behind, ahead, final):
                sum_e(q, u)
                if ahead == 2:
                    turn(q + 1, u)
                if behind:
                    sum_ey(q - 1 + u, 1 - u)

            pe.sem_inc(turned, 2)
            pe.sem_inc(sum_ey_done, 2)
            pe.wait_ge(box_ready, 1)
            images(pe, head, step, lambda level, q, final: sum_ey(q - 1, 1))

        @block.scalar
        def _(act):
            def exponent(q, u):
                n = q * 2 + u
                act.wait_ge(turned, n + 3)
                nc.scalar.activation(e[:, u], ps_t[:, u], ACT.Exp, bias=minus_max[:, 0:1]).then_inc(exp_done, 1)
                act.wait_ge(exp_done, n + 1)
                nc.scalar.copy(e_hi[:, u], e[:, u]).then_inc(e_hi_done, 1)

            def product_hi(q, u):
                n = q * 2 + u
                act.wait_ge(ey_done, n + 3)
                act.wait_ge(sum_ey_done, n + 1)
                nc.scalar.copy(ey_hi[:, u], ey[:, u]).then_inc(ey_hi_done, 1)

            def estimate(q, u):
                n = q * 2 + u
                act.wait_ge(sum_e_done, n + 1)
                nc.scalar.activation(r[:, u], ps_e[:, :], ACT.Ln, bias=eps[:, 0:1]).then_inc(r_done, 1)
                act.wait_ge(r_done, n * 2 + 1)
                nc.scalar.activation(r[:, u], r[:, u], ACT.Exp, scale=-1.0).then_inc(r_done, 1)

            def head(level, final):
                act.wait_ge(batch_max_done, level + 1)
                nc.scalar.mul(minus_max[:, :], batch_max[:, :], -1.0).then_inc(minus_max_done, 1)
                act.wait_ge(minus_max_done, level + 1)
                exponent(level * (B // 2), 0)
                exponent(level * (B // 2), 1)
                product_hi(level * (B // 2), 0)

            def step(level, q, h, u, m, behind, ahead, final):
                estimate(q, u)
                if ahead == 2:
                    exponent(q + 1, u)
                if ahead:
                    product_hi(q + u, 1 - u)
                if m == B - 3:
                    chain.average(act, 0, level)
                if m == B - 2 and not final:
                    chain.pad_next(act, 0, level + 1)

            nc.scalar.preload_act_table_set(EXP_LN)
            act.wait_ge(eps_set, 1)
            act.wait_ge(chain.borders, chain.n_borders)
            chain.pad_first(act, 0)
            images(act, head, step, lambda level, q, final: None)

        @block.gpsimd
        def _(pool):
            def e_low(q, u):
                pool.wait_ge(e_hi_done, q * 2 + u + 1)
                nc.gpsimd.tensor_tensor(e_lo[:, u], e[:, u], e_hi[:, u].bitcast(F32), ALU.subtract).then_inc(e_lo_done, 1)

            def product_low(q, u):
                pool.wait_ge(ey_hi_done, q * 2 + u + 1)
                nc.gpsimd.tensor_tensor(ey_lo[:, u], ey[:, u], ey_hi[:, u].bitcast(F32), ALU.subtract).then_inc(ey_lo_done, 1)

            def head(level, final):
                pool.wait_ge(tile_max_done, level + 1)
                pool.sem_inc(gate, 1)
                nc.gpsimd.partition_all_reduce(batch_max[:, :], tile_max[:, :], P, RMAX).then_inc(batch_max_done, 1)
                e_low(level * (B // 2), 0)
                e_low(level * (B // 2), 1)
                product_low(level * (B // 2), 0)

            def step(level, q, h, u, m, behind, ahead, final):
                if ahead == 2:
                    e_low(q + 1, u)
                if ahead:
                    product_low(q + u, 1 - u)
                if m == 0:
                    chain.box_sums_end(pool, 0, level)
                if m == B - 2 and not final:
                    chain.box_sums_start(pool, 0, level + 1)

            pool.sem_inc(ey_lo_done, 2)
            chain.set_sum_borders()
            nc.gpsimd.memset(eps[:, :], 1e-6).then_inc(eps_set, 1)
            chain.box_sums_start(pool, 0, 0)
            images(pool, head, step, lambda level, q, final: None)

        @block.vector
        def _(dve):
            def product(q, u):
                n = q * 2 + u
                dve.wait_ge(exp_done, n + 1)
                dve.wait_ge(ey_lo_done, n + 1)
                nc.vector.tensor_tensor(ey[:, u], ps_t[:, u], e[:, u], ALU.mult).then_inc(ey_done, 1)

            def residual(q, u):
                n = q * 2 + u
                dve.wait_ge(r_done, n * 2 + 2)
                dve.wait_ge(y_done, n + 1)
                nc.vector.scalar_tensor_tensor(newton[:, u], ps_e[:, :], 1e-6, r[:, u], ALU.add, ALU.mult).then_inc(newton_done, 1)

            def improve(q, u):
                n = q * 2 + u
                dve.wait_ge(newton_done, n * 2 + 3)
                nc.vector.scalar_tensor_tensor(newton[:, u], newton[:, u], 2.0, r[:, u], ALU.subtract, ALU.mult).then_inc(newton_done, 1)

            def divide(q, u):
                n = q * 2 + u
                dve.wait_ge(newton_done, n * 2 + 4)
                dve.wait_ge(sum_ey_done, n + 3)
                dve.wait_ge(stored[u], q * 16 + 16 * (B // 2))
                nc.vector.scalar_tensor_tensor(y_out[:, u], newton[:, u], -1.0, ps_ey[:, :], ALU.mult, ALU.mult).then_inc(y_done, 1)

            def maximum(q, h, u):
                dve.wait_ge(y_done, q * 2 + u + 3)
                nc.vector.reduce_max(rmc[:, bass.ds(h * 2 + u, 1)], y_out[:, u], AX).then_inc(col_max_done, 1)

            def head(level, final):
                dve.wait_ge(col_max_done, level * B + 1)
                nc.vector.reduce_max(tile_max[:, :], rmc[:, :], AX).then_inc(tile_max_done, 1)
                product(level * (B // 2), 0)
                chain.maxima(dve, 0, level)

            def step(level, q, h, u, m, behind, ahead, final):
                residual(q, u)
                if ahead:
                    product(q + u, 1 - u)
                if behind:
                    divide(q - 1 + u, 1 - u)
                improve(q, u)
                if behind and not final:
                    maximum(q - 1 + u, h - 1 + u, 1 - u)
                if m == B - 3:
                    chain.mixture(dve, 0, level)

            def tail(level, q, final):
                divide(q - 1, 1)
                if not final:
                    maximum(q - 1, B // 2 - 1, 1)

            dve.sem_inc(ey_done, 2)
            dve.sem_inc(newton_done, 2)
            dve.sem_inc(y_done, 2)
            dve.sem_inc(col_max_done, 1)
            chain.set_max_borders()
            dve.wait_ge(box_in, 16)
            nc.vector.tensor_copy(box[:, :], box_raw[:, :]).then_inc(box_ready, 1)
            dve.wait_ge(chain.borders, chain.n_borders)
            images(dve, head, step, tail)


def kept_tensors(ctx, nc):
    shapes = {"ident": [P, P], "group": [P, P], "cv1": [P, KT, C], "cv2": [P, KT, C], "cvend": [P, KT, C],
              "c1": [P, KT, C4], "columns": [P, sum(COLUMNS.values())], "minus_half": [P, B * CT]}
    keep = {k: ctx.enter_context(nc.sbuf_tensor("k_" + k, v, F32)) for k, v in shapes.items()}
    at = 0
    for k, n in COLUMNS.items():
        keep[k] = keep["columns"][:, at:at + n]
        at += n
    keep["taps"] = keep["taps"].rearrange("p (s t k) -> p s t k", s=STAGES, t=KT)
    keep["b_taps"] = keep["b_taps"].rearrange("p (s t) -> p s t", s=STAGES)
    for k in ("w1_hi", "w1_lo", "w2_hi", "w2_lo"):
        keep[k] = ctx.enter_context(nc.sbuf_tensor("k_" + k, [P, CT, C], F32R))
    return keep


def constants():
    import numpy as np

    ident = np.eye(P, dtype=np.float32)
    group = np.kron(np.eye(P // GROUP), np.full((GROUP, GROUP), 1.0 / GROUP)).astype(np.float32)
    near_x = np.abs(np.arange(W)[:, None] - np.arange(W)[None, :]) <= 2
    near_r = np.abs(np.arange(P // W)[:, None] + 2 - np.arange(8)[None, :]) <= 2
    return {"ident": ident, "group": group, "box": np.kron(near_r, near_x).astype(np.float32)}


def columns(inputs):
    import numpy as np

    def tiles(a):
        return a.reshape(-1, P).T

    cols = [tiles(inputs["L0_conv_b_" + k]) for k in ("sta", "cv1", "cv2", "cvend", "c1")]
    names = ("dwh", "dwv", "ddwh", "ddwv")
    cols += [inputs["L0_conv_w_" + k].reshape(KT, P, 3).transpose(1, 0, 2).reshape(P, -1) for k in names]
    cols += [tiles(inputs["L0_conv_b_" + k]) for k in names]
    return np.ascontiguousarray(np.concatenate(cols, axis=1))


BEFORE, TILES = 7, N // P
ORDER = (2, 3, 0, 1)


def phase_c(nc, x, out, keep, levels, chain):
    with ExitStack() as ctx:
        def sb(name, shape, dt=F32):
            return ctx.enter_context(nc.sbuf_tensor(name, shape, dt))

        def signal(name, per):
            return Signal(ctx.enter_context(nc.semaphore("c_" + name)), per)

        y2 = sb("y2", [P, LEVELS, N])
        y = sb("y", [P, KT, N])
        a = sb("a", [P, KT, N])
        x1 = sb("x1", [P, CT, N])
        f_hi = sb("f_hi", [P, CT, N], F32R)
        f_lo = sb("f_lo", [P, CT, N], F32R)
        q_hi = sb("q_hi", [P, CT, N], F32R)
        q_lo = sb("q_lo", [P, CT, N], F32R)
        v_hi = sb("v_hi", [P, N // P, C], F32R)
        v_lo = sb("v_lo", [P, N // P, C], F32R)
        prob = sb("prob", [P, N])
        pt_hi = sb("pt_hi", [P, 2, N], F32R)
        pt_lo = sb("pt_lo", [P, 2, N], F32R)
        mixed = sb("mixed", [P, 2, C])
        minus_max = sb("c_minus_max", [P, TILES])
        row_sum = sb("row_sum", [P, TILES])
        row_inv = sb("row_inv", [P, TILES])
        stats = sb("c_stats", [P, CT, 2, 6])
        mv = sb("c_mv", [P, CT, 2])
        gmean = sb("gmean", [P, CT])
        dev = sb("c_dev", [P, CT])
        spread = sb("c_spread", [P, CT])
        rstd = sb("c_rstd", [P, CT])
        shift = sb("c_shift", [P, CT])
        slots = [ctx.enter_context(nc.psum_tensor(f"slot{n}", [P, N], F32)) for n in range(3)]
        ps_o = ctx.enter_context(nc.psum_tensor("ps_o", [P, HALF], F32))
        ps_ot = ctx.enter_context(nc.psum_tensor("ps_ot", [P, HALF], F32))

        y2_loaded = signal("y2_loaded", 16)
        x_loaded = signal("x_loaded", 16)
        stored = signal("stored", 16)
        cv = signal("cv", 2 * CT)
        y_ready = signal("y_ready", KT)
        taps_centre = signal("taps_centre", KT * STAGES)
        taps = signal("taps", 2 * KT * STAGES)
        c1 = signal("c1", KT)
        gated = signal("gated", KT)
        cvend = signal("cvend", CT)
        ended = signal("ended", CT)
        added = signal("added", CT)
        bn = signal("bn", 4 + CT)
        group_mean = signal("group_mean", 1)
        group_var = signal("group_var", 1)
        norm = signal("norm", 6)
        rstd_done = signal("rstd", 1)
        f_done = signal("f", CT)
        f_split = signal("f_split", 2 * CT)
        qv = signal("qv", 4)
        qv_hi = signal("qv_hi", 4)
        qv_lo = signal("qv_lo", 4)
        scores = signal("scores", TILES)
        maxed = signal("maxed", TILES)
        prob_done = signal("prob", TILES)
        turned = signal("turned", TILES)
        pt_hi_done = signal("pt_hi", TILES)
        pt_lo_done = signal("pt_lo", TILES)
        pv = signal("pv", TILES)
        inverse = signal("inverse", TILES)
        mixed_done = signal("mixed", TILES)
        back = signal("back", TILES)
        result = signal("result", TILES)
        stats_gate = ctx.enter_context(nc.semaphore("c_gate"))
        block = ctx.enter_context(nc.Block())

        x_v = x.rearrange("b (t p) h w -> b p t (h w)", p=P)
        out_v = out.rearrange("b (t p) h w -> b p t (h w)", p=P)
        y2_v = levels.rearrange("(l b) p n -> b p l n", b=B)

        def steps(eng, step):
            step(0, True, False, True)
            with eng.Fori(1, B - 1) as i:
                step(i, True, True, True)
            step(B - 1, True, True, False)
            step(B, False, True, False)

        def slot_uses(conv, attn):
            uses = [("cv", k) for k in range(2 * CT)] if conv else []
            if attn:
                uses += [("qv", k) for k in range(4)] + [("s", 0)]
                for t in range(TILES):
                    uses += [("s", t + 1)] * (t + 1 < TILES) + [("t", t)]
            return uses + ([("c1", k) for k in range(KT)] + [("ce", k) for k in range(CT)] if conv else [])

        def slot_plan(conv, attn):
            first = 1 if attn else 0
            return {use: slots[(first + n) % 3] for n, use in enumerate(slot_uses(conv, attn))}

        def stages_of(t):
            return range(BEFORE + t, BEFORE + t + 1)

        def alone(n, attn):
            return n < BEFORE or not attn

        def stage(n):
            c, s = ORDER[n // STAGES], n % STAGES
            w0, w1 = chain.work[:, 0, 0:N], chain.work[:, 1, 0:N]
            src, dst = ((y[:, c], w0), (w0, w1), (w1, w0), (w0, a[:, c]))[s]
            return c, s, src, dst

        @block.sync
        def _(sp):
            def load_chain(i):
                sp.dma_start(chain.stem[:, :], levels[i]).then_inc(chain.loaded.sem, 16)

            def load_y2(i):
                sp.dma_start(y2[:, :, :], y2_v[i, :, 1:LEVELS + 1]).then_inc(y2_loaded.sem, 16)

            def step(i, conv, attn, chained):
                if chained:
                    wait(sp, chain.padded, i, 2)
                    load_chain(i + 1)
                    wait(sp, cv, i, CT)
                    load_y2(i + 1)
                if attn:
                    wait(sp, result, i - 1, TILES)
                    sp.dma_start(out_v[i - 1], x1[:, :, :]).then_inc(stored.sem, 16)
                    wait(sp, stored, i - 1, 16)
                if conv:
                    sp.dma_start(x1[:, :, :], x_v[i]).then_inc(x_loaded.sem, 16)

            load_y2(0)
            steps(sp, step)

        @block.gpsimd
        def _(pool):
            def step(i, conv, attn, chained):
                if attn:
                    wait(pool, norm, i - 1, 4)
                    nc.gpsimd.tensor_tensor(rstd[:, :], spread[:, :], keep["minus_half"][:, 0:CT], ALU.pow).then_inc(rstd_done.sem, 1)
                if chained:
                    wait(pool, chain.done, i, MIX * LEVELS)
                    for level in range(LEVELS):
                        chain.box_sums_start(pool, i + 1, level)
                        chain.box_sums_end(pool, i + 1, level)

            steps(pool, step)

        @block.tensor
        def _(pe):
            def released(use, i, own):
                kind, k = use
                image = i if own else i - 1
                return {"cv": (y_ready, image, k + 1), "c1": (gated, image, k + 1), "ce": (ended, image, k + 1),
                        "qv": (qv_lo, i - 1, k + 1), "s": (prob_done, i - 1, k + 1), "t": (pt_lo_done, i - 1, k + 1)}[kind]

            def step(i, conv, attn, chained):
                uses, slots_of = slot_uses(conv, attn), slot_plan(conv, attn)

                def claim(kind, k):
                    n = uses.index((kind, k))
                    if n >= 3:
                        wait(pe, *released(uses[n - 3], i, True))
                    elif attn:
                        wait(pe, *released(slot_uses(True, False)[n - 3], i, False))
                    return slots_of[kind, k]

                def product(kind, m, weights, inputs, sig, order=range(KT), ready=None):
                    slot = claim(kind, m)
                    for h in range(2):
                        for n, k in enumerate(order):
                            if ready and h == 0:
                                ready(n)
                            last = nc.tensor.matmul(slot[:, h * HALF:(h + 1) * HALF], weights[:, k], inputs(k, h),
                                                    start=(n == 0), stop=(n == KT - 1))
                    last.then_inc(sig.sem, 1)

                def cols(m):
                    return slice(m * P, (m + 1) * P)

                def flat(t):
                    return lambda k, h: t[:, k, h * HALF:(h + 1) * HALF]

                def cat2(k, h):
                    return y2[:, k - 1, h * HALF:(h + 1) * HALF] if k else cat1(k, h)

                def cat1(k, h):
                    return chain.wide[:, k, h * (H // 2):(h + 1) * (H // 2), 2:2 + W]

                def split_product(out, pairs, last_signal=None):
                    parts = [(lh, rh) for lh, ll, rh, rl in pairs] + [(lh, rl) for lh, ll, rh, rl in pairs] \
                        + [(ll, rh) for lh, ll, rh, rl in pairs]
                    for n, (lhs, rhs) in enumerate(parts):
                        last = nc.tensor.matmul(out, lhs, rhs, start=(n == 0), stop=(n == len(parts) - 1))
                    return last

                def score(t):
                    wait(pe, qv_lo, i - 1, 2)
                    slot = claim("s", t)
                    for h in range(2):
                        hs = slice(h * HALF, (h + 1) * HALF)
                        last = split_product(slot[:, hs], [(q_hi[:, k, cols(t)], q_lo[:, k, cols(t)], f_hi[:, k, hs], f_lo[:, k, hs])
                                                           for k in range(CT)])
                    last.then_inc(scores.sem, 1)

                def turn(t):
                    wait(pe, prob_done, i - 1, t + 1)
                    slot = claim("t", t)
                    for m in range(N // P):
                        last = nc.tensor.transpose(slot[:, cols(m)], prob[:, cols(m)], keep["ident"][:, :])
                    last.then_inc(turned.sem, 1)

                def mix(t):
                    wait(pe, pt_lo_done, i - 1, t + 1)
                    wait(pe, qv_lo, i - 1, 4)
                    if t:
                        wait(pe, mixed_done, i - 1, t)
                    split_product(ps_o[:, 0:C], [(pt_hi[:, t % 2, cols(m)], pt_lo[:, t % 2, cols(m)], v_hi[:, m], v_lo[:, m])
                                                 for m in range(N // P)]).then_inc(pv.sem, 1)

                def turn_back(t):
                    wait(pe, mixed_done, i - 1, t + 1)
                    if t:
                        wait(pe, result, i - 1, t)
                    for d in range(CT):
                        last = nc.tensor.transpose(ps_ot[:, cols(d)], mixed[:, t % 2, cols(d)], keep["ident"][:, :])
                    last.then_inc(back.sem, 1)

                def group_sums(rhs, ps, sig):
                    nc.tensor.matmul(ps[:, 0:CT], keep["group"][:, :], rhs, start=True, stop=True).then_inc(sig.sem, 1)

                if conv:
                    wait(pe, y2_loaded, i, 16)
                    wait(pe, chain.padded, i, 1)
                    product("cv", 0, keep["cv2"][:, :, cols(0)], cat2, cv)
                if attn:
                    wait(pe, bn, i - 1, 4 + CT)
                    group_sums(mv[:, :, 0], ps_o, group_mean)
                if conv:
                    product("cv", 1, keep["cv2"][:, :, cols(1)], cat2, cv)
                if attn:
                    wait(pe, norm, i - 1, 3)
                    group_sums(spread[:, :], ps_ot, group_var)
                if conv:
                    for m in range(CT):
                        product("cv", CT + m, keep["cv1"][:, :, cols(m)], cat1, cv,
                                ready=lambda n: wait(pe, chain.done, i, MIX * n) if n else None)
                if attn:
                    wait(pe, f_split, i - 1, 2 * CT)
                    for m in range(CT):
                        slot = claim("qv", m)
                        for h in range(2):
                            hs = slice(h * HALF, (h + 1) * HALF)
                            last = split_product(slot[:, hs], [(keep["w1_hi"][:, k, cols(m)], keep["w1_lo"][:, k, cols(m)],
                                                                f_hi[:, k, hs], f_lo[:, k, hs]) for k in range(CT)])
                        last.then_inc(qv.sem, 1)
                    for half in range(2):
                        slot = claim("qv", 2 + half)
                        for m in range(4):
                            px = cols(4 * half + m)
                            last = split_product(slot[:, m * C:(m + 1) * C], [(f_hi[:, k, px], f_lo[:, k, px], keep["w2_hi"][:, k],
                                                                              keep["w2_lo"][:, k]) for k in range(CT)])
                        last.then_inc(qv.sem, 1)
                    score(0)
                    for t in range(TILES):
                        if t + 1 < TILES:
                            score(t + 1)
                        if t > 1:
                            turn_back(t - 2)
                        if t:
                            mix(t - 1)
                        turn(t)
                    mix(TILES - 1)
                    turn_back(TILES - 2)
                    turn_back(TILES - 1)
                if conv:
                    for m in range(KT):
                        product("c1", m, keep["c1"][:, :, cols(m)], flat(a), c1, order=ORDER,
                                ready=lambda n: wait(pe, taps, i, 2 * STAGES * (n + 1)))
                    for m in range(CT):
                        product("ce", m, keep["cvend"][:, :, cols(m)], flat(y), cvend,
                                ready=lambda n: wait(pe, gated, i, n + 1))

            steps(pe, step)

        @block.scalar
        def _(act):
            def step(i, conv, attn, chained):
                def silu_cv(k):
                    c = ORDER[k]
                    wait(act, cv, i, k + 1)
                    bias = keep["b_cv1"][:, c:c + 1] if c < CT else keep["b_cv2"][:, c - CT:c - CT + 1]
                    nc.scalar.activation(y[:, c], slots_of["cv", k][:, :], ACT.Silu, bias=bias).then_inc(y_ready.sem, 1)

                def centre_tap(n):
                    c, s, src, dst = stage(n)
                    wait(act, taps, i, 2 * n)
                    if s == 0:
                        wait(act, y_ready, i, n // STAGES + 1)
                    if n == 2 * STAGES + 3:
                        wait(act, f_split, i - 1, 2 * CT)
                    nc.scalar.activation(dst, src, ACT.Identity, scale=keep["taps"][:, s, c, 1:2],
                                         bias=keep["b_taps"][:, s, c:c + 1]).then_inc(taps_centre.sem, 1)

                def exponent(t):
                    wait(act, maxed, i - 1, t + 1)
                    if t:
                        wait(act, turned, i - 1, t)
                    nc.scalar.activation(prob[:, :], slots_of["s", t][:, :], ACT.Exp, bias=minus_max[:, t:t + 1],
                                         accum_out=row_sum[:, t:t + 1]).then_inc(prob_done.sem, 1)

                def turned_hi(t):
                    wait(act, turned, i - 1, t + 1)
                    nc.scalar.copy(pt_hi[:, t % 2], slots_of["t", t][:, :]).then_inc(pt_hi_done.sem, 1)

                def scale_mixed(t):
                    wait(act, pv, i - 1, t + 1)
                    wait(act, inverse, i - 1, t + 1)
                    nc.scalar.activation(mixed[:, t % 2], ps_o[:, 0:C], ACT.Copy, scale=row_inv[:, t:t + 1]).then_inc(mixed_done.sem, 1)

                slots_of = slot_plan(conv, attn)
                if conv:
                    silu_cv(0)
                    silu_cv(1)
                if attn:
                    for t in range(CT):
                        wait(act, norm, i - 1, 6)
                        nc.scalar.activation(a[:, t], x1[:, t], ACT.Identity, scale=rstd[:, t:t + 1],
                                             bias=shift[:, t:t + 1]).then_inc(f_done.sem, 1)
                if conv:
                    silu_cv(2)
                    silu_cv(3)
                if attn:
                    for k in range(4):
                        wait(act, qv, i - 1, k + 1)
                        src = slots_of["qv", k][:, :]
                        if k < 2:
                            nc.scalar.activation(q_hi[:, k], src, ACT.Copy, scale=C ** -0.5).then_inc(qv_hi.sem, 1)
                        else:
                            nc.scalar.copy(v_hi[:, 4 * (k - 2):4 * (k - 1)].rearrange("p m c -> p (m c)"), src).then_inc(qv_hi.sem, 1)
                if chained:
                    wait(act, cv, i, 2 * CT)
                    chain.pad_first(act, i + 1)
                if attn:
                    if conv:
                        centre_tap(BEFORE)
                    for t in range(TILES):
                        if t > 1:
                            scale_mixed(t - 2)
                        if t:
                            turned_hi(t - 1)
                        exponent(t)
                        if conv:
                            for n in stages_of(t):
                                if n + 1 < KT * STAGES:
                                    centre_tap(n + 1)
                    turned_hi(TILES - 1)
                    scale_mixed(TILES - 2)
                    scale_mixed(TILES - 1)
                if chained:
                    for level in range(LEVELS - 1):
                        chain.average(act, i + 1, level)
                        chain.pad_next(act, i + 1, level + 1)
                if conv:
                    for m in range(CT):
                        wait(act, cvend, i, m + 1)
                        nc.scalar.activation(a[:, m], slots_of["ce", m][:, :], ACT.Silu, bias=keep["b_cvend"][:, m:m + 1]).then_inc(ended.sem, 1)
                if chained:
                    chain.average(act, i + 1, LEVELS - 1)

            steps(act, step)

        @block.vector
        def _(dve):
            def step(i, conv, attn, chained):
                def outer_taps(n):
                    c, s, src, dst = stage(n)
                    if alone(n, attn):
                        if s == 0:
                            wait(dve, y_ready, i, n // STAGES + 1)
                        if n:
                            wait(dve, taps, i, 2 * n)
                        nc.vector.tensor_scalar(dst, src, keep["taps"][:, s, c, 1:2], keep["b_taps"][:, s, c:c + 1],
                                                ALU.mult, ALU.add).then_inc(taps_centre.sem, 1)
                    wait(dve, taps_centre, i, n + 1)
                    src, dst = image2d(src), image2d(dst)
                    d = 1 if s < 2 else 2
                    for k, tap in ((0, 0), (1, 2)):
                        if tap == 0:
                            far, near = slice(d, W), slice(0, W - d)
                        else:
                            far, near = slice(0, W - d), slice(d, W)
                        o, u = (dst[:, :, far], src[:, :, near]) if s % 2 == 0 else (dst[:, far], src[:, near])
                        if k:
                            wait(dve, taps, i, 2 * n + 1)
                        nc.vector.scalar_tensor_tensor(o, u, keep["taps"][:, s, c, tap:tap + 1], o, ALU.mult, ALU.add).then_inc(taps.sem, 1)

                def turned_lo(t):
                    wait(dve, pt_hi_done, i - 1, t + 1)
                    nc.vector.tensor_tensor(pt_lo[:, t % 2], slots_of["t", t][:, :], pt_hi[:, t % 2].bitcast(F32),
                                            ALU.subtract).then_inc(pt_lo_done.sem, 1)

                def maximum(t):
                    wait(dve, scores, i - 1, t + 1)
                    nc.vector.tensor_reduce(minus_max[:, t:t + 1], slots_of["s", t][:, :], AX, ALU.max, negate=True).then_inc(maxed.sem, 1)

                def invert(t):
                    wait(dve, prob_done, i - 1, t + 1)
                    nc.vector.reciprocal(row_inv[:, t:t + 1], row_sum[:, t:t + 1]).then_inc(inverse.sem, 1)

                def add_attention(t):
                    wait(dve, back, i - 1, t + 1)
                    part = x1[:, :, t * P:(t + 1) * P]
                    nc.vector.tensor_tensor(part, ps_ot[:, 0:C].rearrange("p (d n) -> p d n", d=CT), part, ALU.add).then_inc(result.sem, 1)

                def gate(m):
                    wait(dve, c1, i, m + 1)
                    nc.vector.scalar_tensor_tensor(y[:, m], slots_of["c1", m][:, :], keep["b_c1"][:, m:m + 1], y[:, m],
                                                   ALU.add, ALU.mult).then_inc(gated.sem, 1)

                def add_l0(m):
                    wait(dve, x_loaded, i, 16)
                    wait(dve, ended, i, m + 1)
                    nc.vector.tensor_tensor(x1[:, m], a[:, m], x1[:, m], ALU.add).then_inc(added.sem, 1)
                    wait(dve, added, i, m + 1)
                    for h in range(2):
                        nc.vector.bn_stats(stats[:, m, h, :], x1[:, m, h * HALF:(h + 1) * HALF]).then_inc(bn.sem, 1)

                slots_of = slot_plan(conv, attn)
                before = iter(range(BEFORE if attn else KT * STAGES))
                if attn:
                    small = Steps(dve, norm, i - 1)
                    wait(dve, group_mean, i - 1, 1)
                    small.did(nc.vector.tensor_tensor(dev[:, :], mv[:, :, 0], ps_o[:, 0:CT], ALU.subtract))
                    small.wait()
                    small.did(nc.vector.tensor_tensor(dev[:, :], dev[:, :], dev[:, :], ALU.mult))
                    small.wait()
                    small.did(nc.vector.tensor_tensor(spread[:, :], dev[:, :], mv[:, :, 1], ALU.add))
                if conv:
                    outer_taps(next(before))
                    outer_taps(next(before))
                if attn:
                    wait(dve, group_var, i - 1, 1)
                    small.did(nc.vector.tensor_scalar(spread[:, :], ps_ot[:, 0:CT], 1e-5, None, ALU.add))
                    small.did(nc.vector.tensor_scalar(gmean[:, :], ps_o[:, 0:CT], -1.0, None, ALU.mult))
                    small.wait()
                    wait(dve, rstd_done, i - 1, 1)
                    small.did(nc.vector.tensor_tensor(shift[:, :], gmean[:, :], rstd[:, :], ALU.mult))
                if conv:
                    outer_taps(next(before))
                if attn:
                    for t in range(CT):
                        wait(dve, f_done, i - 1, t + 1)
                        nc.vector.tensor_copy(f_hi[:, t], a[:, t]).then_inc(f_split.sem, 1)
                        wait(dve, f_split, i - 1, 2 * t + 1)
                        nc.vector.tensor_tensor(f_lo[:, t], a[:, t], f_hi[:, t].bitcast(F32), ALU.subtract).then_inc(f_split.sem, 1)
                if conv:
                    for n in before:
                        outer_taps(n)
                        if attn and n == BEFORE - 2:
                            break
                if attn:
                    for k in range(4):
                        if conv and k == 2:
                            outer_taps(next(before))
                        wait(dve, qv_hi, i - 1, k + 1)
                        src = slots_of["qv", k][:, :]
                        if k < 2:
                            nc.vector.scalar_tensor_tensor(q_lo[:, k], src, C ** -0.5, q_hi[:, k].bitcast(F32),
                                                           ALU.mult, ALU.subtract).then_inc(qv_lo.sem, 1)
                        else:
                            m = slice(4 * (k - 2), 4 * (k - 1))
                            nc.vector.tensor_tensor(v_lo[:, m].rearrange("p m c -> p (m c)"), src,
                                                    v_hi[:, m].rearrange("p m c -> p (m c)").bitcast(F32), ALU.subtract).then_inc(qv_lo.sem, 1)
                    maximum(0)
                    for t in range(TILES):
                        if t:
                            turned_lo(t - 1)
                        now = iter(stages_of(t) if conv else ())
                        for n in now:
                            outer_taps(n)
                            break
                        if t + 1 < TILES:
                            maximum(t + 1)
                        for n in now:
                            outer_taps(n)
                        invert(t)
                        if t > 1:
                            add_attention(t - 2)
                    turned_lo(TILES - 1)
                    for n in range(BEFORE + TILES, KT * STAGES if conv else 0):
                        outer_taps(n)
                    add_attention(TILES - 2)
                    add_attention(TILES - 1)
                if chained:
                    wait(dve, taps, i, 2 * KT * STAGES)
                    chain.maxima(dve, i + 1, 0)
                    chain.mixture(dve, i + 1, 0)
                if conv:
                    gate(0)
                if chained:
                    chain.maxima(dve, i + 1, 1)
                if conv:
                    gate(1)
                    gate(2)
                if chained:
                    chain.mixture(dve, i + 1, 1)
                if conv:
                    gate(3)
                if chained:
                    chain.maxima(dve, i + 1, 2)
                if conv:
                    add_l0(0)
                if conv:
                    add_l0(1)
                if chained:
                    chain.mixture(dve, i + 1, 2)
                if conv:
                    wait(dve, bn, i, 4)
                    dve.sem_inc(stats_gate, 1)
                    for m in range(CT):
                        nc.vector.bn_aggr(mv[:, m, :], stats[:, m].rearrange("p h s -> p (h s)")).then_inc(bn.sem, 1)

            steps(dve, step)


def program(nc, x, w, consts, levels, out):
    with ExitStack() as ctx:
        keep = kept_tensors(ctx, nc)
        rmc = ctx.enter_context(nc.sbuf_tensor("rmc", [P, B], F32))
        phase_a(nc, x, w, consts, keep, levels, rmc)
        chain = Chain(ctx, nc)
        phase_b(nc, consts, keep, levels, rmc, chain)
        phase_c(nc, x, out, keep, levels, chain)


def kernel(**inputs):
    import numpy as np
    import concourse.bacc as bacc
    from concourse.bass_utils import run_bass_kernel_spmd

    nc = bacc.Bacc("TRN2", target_bir_lowering=False, num_devices=1)
    arrays = {"x": np.ascontiguousarray(inputs["x"]), "columns": columns(inputs)}
    for k in ("sta", "cv1", "cv2", "cvend", "c1"):
        arrays["w_" + k] = np.ascontiguousarray(inputs["L0_conv_w_" + k][:, :, 0, 0].T)
    for k in ("w1", "w2"):
        arrays["w_" + k] = np.ascontiguousarray(inputs["L1_conv_" + k].T)
    for k, v in constants().items():
        arrays["const_" + k] = v
    aps = {k: nc.dram_tensor("in_" + k, v.shape, F32, kind="ExternalInput").ap() for k, v in arrays.items()}
    levels = nc.dram_tensor("levels", ((LEVELS + 1) * B, P, N), F32, kind="Internal").ap()
    out = nc.dram_tensor("out", (B, C, H, W), F32, kind="ExternalOutput").ap()
    w = {k[2:]: v for k, v in aps.items() if k.startswith("w_")}
    w["columns"] = aps["columns"]
    consts = {k[6:]: v for k, v in aps.items() if k.startswith("const_")}
    program(nc, aps["x"], w, consts, levels, out)
    r = run_bass_kernel_spmd(nc, [{"in_" + k: v for k, v in arrays.items()}], core_ids=[0])
    return r.results[0]["out"]
```

```python
import concourse.bass as bass
from concourse import mybir
from contextlib import ExitStack

F32 = mybir.dt.float32
F32R = mybir.dt.float32r
ALU = mybir.AluOpType
ACT = mybir.ActivationFunctionType
AX = mybir.AxisListType.X
RMAX = bass.bass_isa.ReduceOp.max

P = 128
B = 8
C = 256
CT = C // P
H = W = 32
N = H * W
HALF = 512
C4 = 512
KT = C4 // P
LEVELS = 3
WP = W + 4
GROUP = C // 32
T_POOL = 0.9
K2 = 25
LOWEST = -3.4028235e38
STAGES = 4
COLUMNS = {"b_sta": 1, "b_cv1": CT, "b_cv2": CT, "b_cvend": CT, "b_c1": KT,
           "taps": STAGES * KT * 3, "b_taps": STAGES * KT}
SPLIT = {"w1": (CT, C), "w2": (CT, C), "cvend": (KT, C), "c1": (KT, C4), "cv2": (KT, C)}
EXP_LN, SILU = "natural_log_exp_and_others", "silu_and_others"


class Signal:

    def __init__(self, sem, per, credit=0):
        self.sem, self.per, self.credit = sem, per, credit

    def at(self, image, k):
        return image * self.per + k + self.credit


class Steps:

    def __init__(self, eng, counted, image, k=0):
        self.eng, self.counted, self.image, self.k = eng, counted, image, k

    def did(self, ins):
        self.k += 1
        ins.then_inc(self.counted.sem, 1)

    def wait(self):
        self.eng.wait_ge(self.counted.sem, self.counted.at(self.image, self.k))


MIX = 7


def wait(eng, sig, image, k):
    eng.wait_ge(sig.sem, sig.at(image, k))


def image2d(ap):
    return ap.rearrange("p (h w) -> p h w", w=W)


class Chain:

    def __init__(self, ctx, nc):
        def sb(name, shape):
            return ctx.enter_context(nc.sbuf_tensor(name, shape, F32))

        def counted(name, per):
            return Signal(ctx.enter_context(nc.semaphore("chain_" + name)), per)

        self.nc = nc
        self.stem = sb("chain_in", [P, N])
        self.wide = sb("wide", [P, LEVELS + 1, H, WP])
        self.zero = sb("zero", [P, H, WP])
        self.tall = sb("tall", [P, H + 4, W])
        self.tall_sum = sb("tall_sum", [P, H + 4, W])
        self.sum_a = sb("sum_a", [P, (H + 2) * W])
        self.sum_b = sb("sum_b", [P, H, W])
        self.work_a = sb("work_a", [P, (H + 2) * W])
        self.work_b = sb("work_b", [P, N])
        self.loaded = counted("loaded", 16)
        self.padded = counted("padded", 1 + LEVELS)
        self.done = counted("done", MIX * LEVELS)
        self.summed = counted("summed", 6 * LEVELS)
        self.averaged = counted("averaged", LEVELS)
        self.borders = ctx.enter_context(nc.semaphore("chain_borders"))
        self.gate = ctx.enter_context(nc.semaphore("chain_gate"))
        self.n_borders = 2 + 2 * LEVELS + 1

    def inner(self, k):
        return self.wide[:, k, :, 2:2 + W]

    def set_sum_borders(self):
        self.nc.gpsimd.memset(self.zero[:, :, :], 0.0).then_inc(self.borders, 1)
        self.nc.gpsimd.memset(self.tall_sum[:, :, :], 0.0).then_inc(self.borders, 1)

    def set_max_borders(self):
        for k in range(LEVELS):
            self.nc.vector.memset(self.wide[:, k, :, 0:2], LOWEST).then_inc(self.borders, 1)
            self.nc.vector.memset(self.wide[:, k, :, 2 + W:WP], LOWEST).then_inc(self.borders, 1)
        self.nc.vector.memset(self.tall[:, :, :], LOWEST).then_inc(self.borders, 1)

    def pad_first(self, act, i):
        wait(act, self.loaded, i, 16)
        self.nc.scalar.copy(self.inner(0), image2d(self.stem[:, :])).then_inc(self.padded.sem, 1)
        self.nc.scalar.copy(self.zero[:, :, 2:2 + W], image2d(self.stem[:, :])).then_inc(self.padded.sem, 1)

    def pad_next(self, act, i, level):
        wait(act, self.done, i, MIX * level)
        act.sem_inc(self.gate, 1)
        self.nc.scalar.copy(self.zero[:, :, 2:2 + W], self.inner(level)).then_inc(self.padded.sem, 1)

    def average(self, act, i, level):
        wait(act, self.summed, i, 6 * (level + 1))
        self.nc.scalar.mul(self.sum_b[:, :, :], self.sum_b[:, :, :], (1.0 - T_POOL) / K2).then_inc(self.averaged.sem, 1)

    def box_sums_start(self, pool, i, level):
        wait(pool, self.padded, i, 2 + level)
        own = Steps(pool, self.summed, i, 6 * level)
        sa = self.sum_a[:, :].rearrange("p (h w) -> p h w", w=WP - 2)
        self.add(own, sa, self.zero[:, :, 0:WP - 2], self.zero[:, :, 1:WP - 1], first=True)
        self.add(own, self.sum_b[:, :, :], sa[:, :, 0:W], sa[:, :, 2:W + 2])
        self.add(own, self.tall_sum[:, 2:H + 2], self.sum_b[:, :, :], self.zero[:, :, 4:WP])
        self.add(own, self.sum_rows(), self.tall_sum[:, 0:H + 2], self.tall_sum[:, 1:H + 3])

    def box_sums_end(self, pool, i, level):
        own = Steps(pool, self.summed, i, 6 * level + 4)
        sv = self.sum_rows()
        self.add(own, self.sum_b[:, :, :], sv[:, 0:H], sv[:, 2:H + 2])
        self.add(own, self.sum_b[:, :, :], self.sum_b[:, :, :], self.tall_sum[:, 4:H + 4])

    def add(self, own, out, in0, in1, first=False):
        if not first:
            own.wait()
        own.did(self.nc.gpsimd.tensor_tensor(out, in0, in1, ALU.add))

    def sum_rows(self):
        return self.sum_a[:, :].rearrange("p (h w) -> p h w", w=W)

    def maxima(self, dve, i, level):
        self.row_maxima(dve, i, level)
        self.column_maxima(dve, i, level)

    def row_maxima(self, dve, i, level):
        wait(dve, self.padded, i, 1)
        own = Steps(dve, self.done, i, MIX * level)
        mh = self.work_a[:, :].rearrange("p (h w) -> p h w", w=WP - 2)
        m4 = image2d(self.work_b[:, :])
        src = self.wide[:, level]
        self.larger(own, mh, src[:, :, 0:WP - 2], src[:, :, 1:WP - 1], first=True)
        self.larger(own, m4, mh[:, :, 0:W], mh[:, :, 2:W + 2])
        self.larger(own, self.tall[:, 2:H + 2], m4, src[:, :, 4:WP])

    def column_maxima(self, dve, i, level):
        own = Steps(dve, self.done, i, MIX * level + 3)
        mv = self.work_a[:, :].rearrange("p (h w) -> p h w", w=W)
        m4 = image2d(self.work_b[:, :])
        self.larger(own, mv, self.tall[:, 0:H + 2], self.tall[:, 1:H + 3])
        self.larger(own, m4, mv[:, 0:H], mv[:, 2:H + 2])
        self.larger(own, m4, m4, self.tall[:, 4:H + 4])

    def larger(self, own, out, in0, in1, first=False):
        if not first:
            own.wait()
        own.did(self.nc.vector.tensor_tensor(out, in0, in1, ALU.max))

    def mixture(self, dve, i, level):
        wait(dve, self.averaged, i, level + 1)
        own = Steps(dve, self.done, i, MIX * level + 6)
        own.wait()
        own.did(self.nc.vector.scalar_tensor_tensor(self.inner(level + 1), image2d(self.work_b[:, :]), T_POOL,
                                                    self.sum_b[:, :, :], ALU.mult, ALU.add))
        own.wait()


class Pooled:

    ORDER = (0, 2, 1, 3)

    def __init__(self, ctx, nc, levels, chain):
        self.nc, self.chain = nc, chain
        self.second = ctx.enter_context(nc.sbuf_tensor("pooled", [P, N], F32))
        self.shared = ctx.enter_context(nc.sbuf_tensor("q_all", [P, KT, N], F32R))
        self.other = None
        self.second_in = Signal(ctx.enter_context(nc.semaphore("pooled_second_in")), 16)
        self.others_in = Signal(ctx.enter_context(nc.semaphore("pooled_others_in")), 16)
        self.stored = [ctx.enter_context(nc.semaphore(f"stored{u}")) for u in range(2)]
        self.hi_done = Signal(ctx.enter_context(nc.semaphore("pooled_hi")), KT)
        self.lo_done = Signal(ctx.enter_context(nc.semaphore("pooled_lo")), KT)
        self.levels = levels.rearrange("(l b) p n -> b p l n", b=B)

    def load_second(self, sp, i):
        sp.dma_start(self.second[:, :], self.levels[i, :, 2]).then_inc(self.second_in.sem, 16)

    def load_others(self, sp, i):
        sp.dma_start(self.shared[:, 2:4].bitcast(F32), self.levels[i, :, 1:LEVELS + 1:2]).then_inc(self.others_in.sem, 16)

    def hi(self, k):
        return {0: self.other[:, 2], 1: self.shared[:, 0], 2: self.other[:, 0], 3: self.shared[:, 1]}[k]

    def lo(self, k):
        return {0: self.other[:, 3], 1: self.shared[:, 2], 2: self.other[:, 1], 3: self.shared[:, 3]}[k]

    def raw(self, k):
        if k == 0:
            return self.chain.inner(0)
        return image2d(self.second[:, :] if k == 2 else self.lo(k).bitcast(F32))

    def split_hi(self, act, i, n):
        k = self.ORDER[n]
        if k:
            wait(act, self.second_in if k == 2 else self.others_in, i, 16)
        self.nc.scalar.copy(image2d(self.hi(k)), self.raw(k)).then_inc(self.hi_done.sem, 1)

    def split_lo(self, dve, i, n):
        k = self.ORDER[n]
        wait(dve, self.hi_done, i, n + 1)
        self.nc.vector.tensor_tensor(image2d(self.lo(k)), self.raw(k), image2d(self.hi(k)).bitcast(F32),
                                     ALU.subtract).then_inc(self.lo_done.sem, 1)


def phase_a(nc, x, w, consts, keep, levels, rmc, box, chain, pooled):
    with ExitStack() as ctx:
        def sb(name, shape, dt=F32):
            return ctx.enter_context(nc.sbuf_tensor(name, shape, dt))

        def sem(name):
            return ctx.enter_context(nc.semaphore(name))

        x_all = sb("x_all", [P, B, CT, N])
        xn = sb("xn", [P, 2, CT, N])
        w_sta = sb("w_sta", [P, CT, P])
        box_raw = sb("box_raw", [P, 8 * W])
        stem = (pooled.second, chain.work_b)
        raw, at = {}, 0
        space = x_all[:, 0:3].rearrange("p b t n -> p (b t n)")
        for k, (tiles, cols) in SPLIT.items():
            raw[k] = space[:, at:at + tiles * cols].rearrange("p (t o) -> p t o", t=tiles)
            at += tiles * cols
        stats = sb("stats", [P, B, CT, 2, 6])
        mv = sb("mv", [P, B * CT, 2])
        dev = sb("dev", [P, B * CT])
        spread = sb("spread", [P, B * CT])
        rstd = sb("rstd", [P, B * CT])
        shift = sb("shift", [P, B * CT])
        ps = ctx.enter_context(nc.psum_tensor("ps_a", [P, 2, N], F32))
        ps_mean = ctx.enter_context(nc.psum_tensor("ps_mean", [P, HALF], F32))
        ps_var = ctx.enter_context(nc.psum_tensor("ps_var", [P, HALF], F32))

        x_in = [sem(f"a_x_in{i}") for i in range(B)]
        sta_in, weights_in, box_in = sem("a_sta_in"), sem("a_weights_in"), sem("a_box_in")
        stats_done = sem("a_stats_done")
        mv_done = sem("a_mv_done")
        mean_done = sem("a_mean_done")
        dev_done = sem("a_dev_done")
        var_done = sem("a_var_done")
        eps_done = sem("a_eps_done")
        rstd_done = sem("a_rstd_done")
        shift_done = sem("a_shift_done")
        split_done, low_done = sem("a_split_done"), sem("a_low_done")
        xn_done = sem("a_xn_done")
        sta_done = sem("a_sta_done")
        stem_done = sem("a_stem_done")
        max_done = sem("a_max_done")
        box_ready = sem("a_box_ready")
        stored = pooled.stored
        block = ctx.enter_context(nc.Block())

        x_v = x.rearrange("b (t p) h w -> b p t (h w)", p=P)
        group = B // 2

        def of_group(g):
            return slice(g * group * CT, (g + 1) * group * CT)

        def rows(k):
            return w[k].rearrange("(t p) o -> p t o", p=P)

        @block.sync
        def _(sp):
            for i in range(B):
                sp.dma_start(x_all[:, i], x_v[i]).then_inc(x_in[i], 16)
            sp.dma_start(box_raw[:, :], consts["box"]).then_inc(box_in, 16)
            sp.dma_start(keep["cv1"][:, :, :], rows("cv1")).then_inc(weights_in, 16)
            sp.wait_ge(xn_done, 3 * CT)
            for k in SPLIT:
                sp.dma_start(raw[k], rows(k)).then_inc(weights_in, 16)

            def store(n, u):
                sp.wait_ge(stem_done, n + 3)
                sp.dma_start(levels[n], stem[u][:, :]).then_inc(stored[u], 16)

            store(0, 0)
            store(1, 1)
            sp.wait_ge(stored[0], 16)
            sp.dma_start(chain.stem[:, :], levels[0]).then_inc(chain.loaded.sem, 16)
            with sp.Fori(1, B // 2) as pair:
                for u in range(2):
                    store(pair * 2 + u, u)

        @block.scalar
        def _(act):
            loads = [(keep["group"][:, :], consts["group"]), (w_sta[:, :, :], rows("sta")),
                     (keep["columns"][:, :], w["columns"]), (keep["ident"][:, :], consts["ident"])]
            for dst, src in loads:
                act.dma_start(dst, src).then_inc(sta_in, 16)
            nc.scalar.preload_act_table_set(SILU)
            act.wait_ge(sta_in, 16 * len(loads))
            act.sem_inc(stem_done, 2)

            def silu(n, u):
                act.wait_ge(sta_done, n + 3)
                if u is not n:
                    act.wait_ge(max_done, n - 1)
                nc.scalar.activation(stem[u][:, :], ps[:, u], ACT.Silu, bias=keep["b_sta"]).then_inc(stem_done, 1)

            silu(0, 0)
            silu(1, 1)
            act.wait_ge(weights_in, 16 * (1 + len(SPLIT)))
            for k in SPLIT:
                nc.scalar.copy(keep[k + "_hi"][:, :, :], raw[k]).then_inc(split_done, 1)
            act.wait_ge(chain.borders, chain.n_borders)
            chain.pad_first(act, 0)
            with act.Fori(1, B // 2) as pair:
                for u in range(2):
                    act.wait_ge(stored[u], pair * 16)
                    silu(pair * 2 + u, u)

        @block.tensor
        def _(pe):
            def statistics(g):
                pe.wait_ge(mv_done, (g + 1) * group * CT)
                nc.tensor.matmul(ps_mean[:, of_group(g)], keep["group"][:, :], mv[:, of_group(g), 0],
                                 start=True, stop=True).then_inc(mean_done, 1)
                pe.wait_ge(dev_done, 3 * (g + 1))
                nc.tensor.matmul(ps_var[:, of_group(g)], keep["group"][:, :], spread[:, of_group(g)],
                                 start=True, stop=True).then_inc(var_done, 1)

            def convolve(n, u):
                pe.wait_ge(xn_done, CT * n + CT)
                pe.wait_ge(stem_done, n + 1)
                for h in range(2):
                    for k in range(CT):
                        last = nc.tensor.matmul(ps[:, u, h * HALF:(h + 1) * HALF], w_sta[:, k, :],
                                                xn[:, u, k, h * HALF:(h + 1) * HALF], start=(k == 0), stop=(k == CT - 1))
                last.then_inc(sta_done, 1)

            pe.sem_inc(sta_done, 2)
            pe.wait_ge(stem_done, 2)
            statistics(0)
            for n in range(group - 1):
                convolve(n, n % 2)
            statistics(1)
            convolve(group - 1, (group - 1) % 2)
            with pe.Fori(group // 2, B // 2) as pair:
                for u in range(2):
                    convolve(pair * 2 + u, u)

        @block.gpsimd
        def _(pool):
            nc.gpsimd.memset(keep["minus_half"][:, :], -0.5).then_inc(rstd_done, 1)
            chain.set_sum_borders()
            pool.wait_ge(rstd_done, 1)

            def inverse_deviations(g):
                pool.wait_ge(eps_done, g + 1)
                nc.gpsimd.tensor_tensor(rstd[:, of_group(g)], spread[:, of_group(g)], keep["minus_half"][:, of_group(g)],
                                        ALU.pow).then_inc(rstd_done, 1)

            def low_parts(names):
                for k in names:
                    pool.wait_ge(split_done, list(SPLIT).index(k) + 1)
                    nc.gpsimd.tensor_tensor(keep[k + "_lo"][:, :, :], raw[k], keep[k + "_hi"][:, :, :].bitcast(F32),
                                            ALU.subtract).then_inc(low_done, 1)

            inverse_deviations(0)
            low_parts(("w1", "w2"))
            inverse_deviations(1)
            chain.box_sums_start(pool, 0, 0)
            low_parts(("cvend", "c1", "cv2"))

        @block.vector
        def _(dve):
            def take_stats(i):
                dve.wait_ge(x_in[i], 16)
                for t in range(CT):
                    for h in range(2):
                        nc.vector.bn_stats(stats[:, i, t, h, :], x_all[:, i, t, h * HALF:(h + 1) * HALF]).then_inc(stats_done, 1)

            def deviations(g):
                part = of_group(g)
                dve.wait_ge(stats_done, (g + 1) * group * CT * 2)
                for i in range(g * group, (g + 1) * group):
                    for t in range(CT):
                        nc.vector.bn_aggr(mv[:, i * CT + t, :], stats[:, i, t].rearrange("p h s -> p (h s)")).then_inc(mv_done, 1)
                dve.wait_ge(mean_done, g + 1)
                dve.wait_ge(mv_done, (g + 1) * group * CT)
                nc.vector.tensor_tensor(dev[:, part], mv[:, part, 0], ps_mean[:, part], ALU.subtract).then_inc(dev_done, 1)
                dve.wait_ge(dev_done, 3 * g + 1)
                nc.vector.tensor_tensor(dev[:, part], dev[:, part], dev[:, part], ALU.mult).then_inc(dev_done, 1)
                dve.wait_ge(dev_done, 3 * g + 2)
                nc.vector.tensor_tensor(spread[:, part], dev[:, part], mv[:, part, 1], ALU.add).then_inc(dev_done, 1)
                dve.wait_ge(var_done, g + 1)
                nc.vector.tensor_scalar(spread[:, part], ps_var[:, part], 1e-5, None, ALU.add).then_inc(eps_done, 1)

            def shifts(g):
                part = of_group(g)
                dve.wait_ge(rstd_done, g + 2)
                nc.vector.scalar_tensor_tensor(shift[:, part], ps_mean[:, part], -1.0, rstd[:, part], ALU.mult, ALU.mult).then_inc(shift_done, 1)
                dve.wait_ge(shift_done, g + 1)

            def normalise(n):
                u = n % 2
                dve.wait_ge(sta_done, n + 1)
                for t in range(CT):
                    at = n * CT + t
                    nc.vector.tensor_scalar(xn[:, u, t], x_all[:, n, t], rstd[:, at:at + 1], shift[:, at:at + 1],
                                            ALU.mult, ALU.add).then_inc(xn_done, 1)

            def maximum(n):
                dve.wait_ge(stem_done, n + 3)
                nc.vector.reduce_max(rmc[:, n:n + 1], stem[n % 2][:, :], AX).then_inc(max_done, 1)

            chain.set_max_borders()
            for i in range(group):
                take_stats(i)
            deviations(0)
            take_stats(group)
            shifts(0)
            normalise(0)
            normalise(1)
            for i in range(group + 1, B):
                take_stats(i)
                if i - group + 1 < group:
                    normalise(i - group + 1)
            deviations(1)
            maximum(0)
            shifts(1)
            normalise(group)
            maximum(1)
            for n in range(group + 1, B):
                maximum(n - 3)
                normalise(n)
            dve.wait_ge(box_in, 16)
            nc.vector.tensor_copy(box[:, :], box_raw[:, :]).then_inc(box_ready, 1)
            for n in range(B - 3, B):
                maximum(n)


def phase_b(nc, keep, levels, rmc, box, chain, pooled):
    with ExitStack() as ctx:
        def sb(name, shape, dt=F32):
            return ctx.enter_context(nc.sbuf_tensor(name, shape, dt))

        def sem(name):
            return ctx.enter_context(nc.semaphore("b_" + name))

        y_in = sb("y_in", [P, 2, N])
        e = sb("e", [P, 2, N])
        ey = sb("ey", [P, 2, N])
        e_hi = sb("e_hi", [P, 2, N], F32R)
        e_lo = sb("e_lo", [P, 2, N], F32R)
        ey_hi = sb("ey_hi", [P, 2, N], F32R)
        ey_lo = sb("ey_lo", [P, 2, N], F32R)
        r = sb("r", [P, 2, N])
        newton = sb("newton", [P, 2, N])
        y_out = sb("y_out", [P, 2, N])
        tile_max = sb("tile_max", [P, 1])
        batch_max = sb("batch_max", [P, 1])
        minus_max = sb("minus_max", [P, 1])
        eps = sb("eps", [P, 1])
        ps_t = ctx.enter_context(nc.psum_tensor("ps_t", [P, 2, N], F32))
        ps_e = ctx.enter_context(nc.psum_tensor("ps_e", [P, N], F32))
        ps_ey = ctx.enter_context(nc.psum_tensor("ps_ey", [P, N], F32))

        loaded = [sem(f"loaded{u}") for u in range(2)]
        turned = sem("turned")
        exp_done, e_hi_done, e_lo_done = sem("exp_done"), sem("e_hi_done"), sem("e_lo_done")
        ey_done, ey_hi_done, ey_lo_done = sem("ey_done"), sem("ey_hi_done"), sem("ey_lo_done")
        sum_e_done, sum_ey_done = sem("sum_e_done"), sem("sum_ey_done")
        r_done, newton_done, y_done = sem("r_done"), sem("newton_done"), sem("y_done")
        col_max_done, tile_max_done = sem("col_max_done"), sem("tile_max_done")
        batch_max_done, minus_max_done = sem("batch_max_done"), sem("minus_max_done")
        eps_set, gate = sem("eps_set"), sem("gate")
        stored = pooled.stored
        block = ctx.enter_context(nc.Block())

        def images(eng, head, step, tail, unroll_final=False):
            def level_of(level, final):
                def one(h, u, m=None):
                    step(level, level * (B // 2) + h, h, u, m, behind=m != 0, ahead=2 if m is None else min(2, B - 1 - m), final=final)

                head(level, final)
                if final and unroll_final:
                    for m in range(B):
                        one(m // 2, m % 2, m)
                else:
                    one(0, 0, 0)
                    with eng.Fori(0, B // 2 - 2) as h:
                        one(h, 1)
                        one(h + 1, 0)
                    for m in range(B - 3, B):
                        one(m // 2, m % 2, m)
                tail(level, level * (B // 2) + B // 2, final)

            with eng.Fori(0, LEVELS - 1) as level:
                level_of(level, False)
            level_of(LEVELS - 1, True)

        @block.sync
        def _(sp):
            def load(q, u):
                n = q * 2 + u
                sp.wait_ge(turned, n + 1)
                sp.wait_ge(stored[u], q * 16 + 16)
                sp.dma_start(y_in[:, u], levels[n]).then_inc(loaded[u], 16)

            def store(q, u):
                n = q * 2 + u
                sp.wait_ge(y_done, n + 3)
                sp.dma_start(levels[n + B], y_out[:, u]).then_inc(stored[u], 16)

            def head(level, final):
                for u in range(2):
                    load(level * (B // 2) + 1, u)
                if final:
                    pooled.load_second(sp, 0)

            def step(level, q, h, u, m, behind, ahead, final):
                if m is None or m < (B - 4 if final else B - 2):
                    load(q + 2, u)
                if final and m == 3:
                    sp.wait_ge(stored[0], 16 * ((B // 2) * LEVELS + 1))
                    pooled.load_others(sp, 0)
                if behind:
                    store(q - 1 + u, 1 - u)

            for u in range(2):
                load(0, u)
            images(sp, head, step, lambda level, q, final: store(q - 1, 1), unroll_final=True)

        @block.tensor
        def _(pe):
            def turn(q, u):
                n = q * 2 + u
                pe.wait_ge(loaded[u], q * 16 + 16)
                pe.wait_ge(ey_done, n + 1)
                for k in range(N // P):
                    last = nc.tensor.transpose(ps_t[:, u, k * P:(k + 1) * P], y_in[:, u, k * P:(k + 1) * P], keep["ident"][:, :])
                last.then_inc(turned, 1)

            def box_sum(out, hi, lo, lo_ready):
                rows, bank = P // W, HALF // W
                started = set()
                for part in (hi, lo):
                    if part is lo:
                        pe.wait_ge(*lo_ready)
                    for k in range(N // P):
                        first, end = max(rows * k - 2, 0), min(rows * k + rows + 2, H)
                        for b in range(first // bank, (end - 1) // bank + 1):
                            r0, r1 = max(first, b * bank), min(end, (b + 1) * bank)
                            c0 = (r0 - (rows * k - 2)) * W
                            last = nc.tensor.matmul(out[:, r0 * W:r1 * W], part[:, k * P:(k + 1) * P],
                                                    box[:, c0:c0 + (r1 - r0) * W], start=(b not in started),
                                                    stop=(part is lo and k == N // P - 1), skip_group_check=True)
                            started.add(b)
                return last

            def sum_e(q, u):
                n = q * 2 + u
                pe.wait_ge(e_hi_done, n + 1)
                pe.wait_ge(newton_done, n * 2 + 1)
                box_sum(ps_e, e_hi[:, u], e_lo[:, u], (e_lo_done, n + 1)).then_inc(sum_e_done, 1)

            def sum_ey(q, u):
                n = q * 2 + u
                pe.wait_ge(ey_hi_done, n + 1)
                pe.wait_ge(y_done, n + 2)
                box_sum(ps_ey, ey_hi[:, u], ey_lo[:, u], (ey_lo_done, n + 3)).then_inc(sum_ey_done, 1)

            def head(level, final):
                for u in range(2):
                    turn(level * (B // 2), u)

            def step(level, q, h, u, m, behind, ahead, final):
                sum_e(q, u)
                if ahead == 2:
                    turn(q + 1, u)
                if behind:
                    sum_ey(q - 1 + u, 1 - u)

            pe.sem_inc(turned, 2)
            pe.sem_inc(sum_ey_done, 2)
            images(pe, head, step, lambda level, q, final: sum_ey(q - 1, 1))

        @block.scalar
        def _(act):
            def exponent(q, u):
                n = q * 2 + u
                act.wait_ge(turned, n + 3)
                nc.scalar.activation(e[:, u], ps_t[:, u], ACT.Exp, bias=minus_max[:, 0:1]).then_inc(exp_done, 1)
                act.wait_ge(exp_done, n + 1)
                nc.scalar.copy(e_hi[:, u], e[:, u]).then_inc(e_hi_done, 1)

            def product_hi(q, u):
                n = q * 2 + u
                act.wait_ge(ey_done, n + 3)
                act.wait_ge(sum_ey_done, n + 1)
                nc.scalar.copy(ey_hi[:, u], ey[:, u]).then_inc(ey_hi_done, 1)

            def estimate(q, u):
                n = q * 2 + u
                act.wait_ge(sum_e_done, n + 1)
                nc.scalar.activation(r[:, u], ps_e[:, :], ACT.Ln, bias=eps[:, 0:1]).then_inc(r_done, 1)
                act.wait_ge(r_done, n * 2 + 1)
                nc.scalar.activation(r[:, u], r[:, u], ACT.Exp, scale=-1.0).then_inc(r_done, 1)

            def head(level, final):
                act.wait_ge(batch_max_done, level + 1)
                nc.scalar.mul(minus_max[:, :], batch_max[:, :], -1.0).then_inc(minus_max_done, 1)
                act.wait_ge(minus_max_done, level + 1)
                exponent(level * (B // 2), 0)
                exponent(level * (B // 2), 1)
                product_hi(level * (B // 2), 0)

            def step(level, q, h, u, m, behind, ahead, final):
                estimate(q, u)
                if ahead == 2:
                    exponent(q + 1, u)
                if ahead:
                    product_hi(q + u, 1 - u)
                if m == B - 3:
                    chain.average(act, 0, level)
                if m == B - 2 and not final:
                    chain.pad_next(act, 0, level + 1)

            nc.scalar.preload_act_table_set(EXP_LN)
            act.wait_ge(eps_set, 1)
            images(act, head, step, lambda level, q, final: None)

        @block.gpsimd
        def _(pool):
            def e_low(q, u):
                pool.wait_ge(e_hi_done, q * 2 + u + 1)
                nc.gpsimd.tensor_tensor(e_lo[:, u], e[:, u], e_hi[:, u].bitcast(F32), ALU.subtract).then_inc(e_lo_done, 1)

            def product_low(q, u):
                pool.wait_ge(ey_hi_done, q * 2 + u + 1)
                nc.gpsimd.tensor_tensor(ey_lo[:, u], ey[:, u], ey_hi[:, u].bitcast(F32), ALU.subtract).then_inc(ey_lo_done, 1)

            def head(level, final):
                pool.wait_ge(tile_max_done, level + 1)
                pool.sem_inc(gate, 1)
                nc.gpsimd.partition_all_reduce(batch_max[:, :], tile_max[:, :], P, RMAX).then_inc(batch_max_done, 1)
                e_low(level * (B // 2), 0)
                e_low(level * (B // 2), 1)
                product_low(level * (B // 2), 0)

            def step(level, q, h, u, m, behind, ahead, final):
                if ahead == 2:
                    e_low(q + 1, u)
                if ahead:
                    product_low(q + u, 1 - u)
                if m == 0:
                    chain.box_sums_end(pool, 0, level)
                if m == B - 2 and not final:
                    chain.box_sums_start(pool, 0, level + 1)

            pool.sem_inc(ey_lo_done, 2)
            nc.gpsimd.memset(eps[:, :], 1e-6).then_inc(eps_set, 1)
            images(pool, head, step, lambda level, q, final: None)

        @block.vector
        def _(dve):
            def product(q, u):
                n = q * 2 + u
                dve.wait_ge(exp_done, n + 1)
                dve.wait_ge(ey_lo_done, n + 1)
                nc.vector.tensor_tensor(ey[:, u], ps_t[:, u], e[:, u], ALU.mult).then_inc(ey_done, 1)

            def residual(q, u):
                n = q * 2 + u
                dve.wait_ge(r_done, n * 2 + 2)
                dve.wait_ge(y_done, n + 1)
                nc.vector.scalar_tensor_tensor(newton[:, u], ps_e[:, :], 1e-6, r[:, u], ALU.add, ALU.mult).then_inc(newton_done, 1)

            def improve(q, u):
                n = q * 2 + u
                dve.wait_ge(newton_done, n * 2 + 3)
                nc.vector.scalar_tensor_tensor(newton[:, u], newton[:, u], 2.0, r[:, u], ALU.subtract, ALU.mult).then_inc(newton_done, 1)

            def divide(q, u):
                n = q * 2 + u
                dve.wait_ge(newton_done, n * 2 + 4)
                dve.wait_ge(sum_ey_done, n + 3)
                dve.wait_ge(stored[u], q * 16 + 16 * (B // 2))
                nc.vector.scalar_tensor_tensor(y_out[:, u], newton[:, u], -1.0, ps_ey[:, :], ALU.mult, ALU.mult).then_inc(y_done, 1)

            def maximum(q, h, u):
                dve.wait_ge(y_done, q * 2 + u + 3)
                nc.vector.reduce_max(rmc[:, bass.ds(h * 2 + u, 1)], y_out[:, u], AX).then_inc(col_max_done, 1)

            def head(level, final):
                dve.wait_ge(col_max_done, level * B + 1)
                nc.vector.reduce_max(tile_max[:, :], rmc[:, :], AX).then_inc(tile_max_done, 1)
                product(level * (B // 2), 0)
                chain.row_maxima(dve, 0, level)

            def step(level, q, h, u, m, behind, ahead, final):
                residual(q, u)
                if ahead:
                    product(q + u, 1 - u)
                if behind:
                    divide(q - 1 + u, 1 - u)
                improve(q, u)
                if m == 0:
                    chain.column_maxima(dve, 0, level)
                if behind and not final:
                    maximum(q - 1 + u, h - 1 + u, 1 - u)
                if m == B - 3:
                    chain.mixture(dve, 0, level)

            def tail(level, q, final):
                divide(q - 1, 1)
                if not final:
                    maximum(q - 1, B // 2 - 1, 1)

            dve.sem_inc(ey_done, 2)
            dve.sem_inc(newton_done, 2)
            dve.sem_inc(y_done, 2)
            dve.sem_inc(col_max_done, 1)
            images(dve, head, step, tail)


def kept_tensors(ctx, nc):
    shapes = {"ident": [P, P], "group": [P, P], "cv1": [P, KT, C],
              "columns": [P, sum(COLUMNS.values())], "minus_half": [P, B * CT]}
    keep = {k: ctx.enter_context(nc.sbuf_tensor("k_" + k, v, F32)) for k, v in shapes.items()}
    at = 0
    for k, n in COLUMNS.items():
        keep[k] = keep["columns"][:, at:at + n]
        at += n
    keep["taps"] = keep["taps"].rearrange("p (s t k) -> p s t k", s=STAGES, t=KT)
    keep["b_taps"] = keep["b_taps"].rearrange("p (s t) -> p s t", s=STAGES)
    for k, (tiles, cols) in SPLIT.items():
        for part in ("_hi", "_lo"):
            keep[k + part] = ctx.enter_context(nc.sbuf_tensor("k_" + k + part, [P, tiles, cols], F32R))
    return keep


def constants():
    import numpy as np

    ident = np.eye(P, dtype=np.float32)
    group = np.kron(np.eye(P // GROUP), np.full((GROUP, GROUP), 1.0 / GROUP)).astype(np.float32)
    near_x = np.abs(np.arange(W)[:, None] - np.arange(W)[None, :]) <= 2
    near_r = np.abs(np.arange(P // W)[:, None] + 2 - np.arange(8)[None, :]) <= 2
    return {"ident": ident, "group": group, "box": np.kron(near_r, near_x).astype(np.float32)}


def columns(inputs):
    import numpy as np

    def tiles(a):
        return a.reshape(-1, P).T

    cols = [tiles(inputs["L0_conv_b_" + k]) for k in ("sta", "cv1", "cv2", "cvend", "c1")]
    names = ("dwh", "dwv", "ddwh", "ddwv")
    cols += [inputs["L0_conv_w_" + k].reshape(KT, P, 3).transpose(1, 0, 2).reshape(P, -1) for k in names]
    cols += [tiles(inputs["L0_conv_b_" + k]) for k in names]
    return np.ascontiguousarray(np.concatenate(cols, axis=1))


TILES = N // P
BEFORE = KT * STAGES - TILES
ORDER = (2, 3, 0, 1)


def phase_c(nc, x, out, keep, levels, chain, pooled):
    with ExitStack() as ctx:
        def sb(name, shape, dt=F32):
            return ctx.enter_context(nc.sbuf_tensor(name, shape, dt))

        def signal(name, per, credit=0):
            return Signal(ctx.enter_context(nc.semaphore("c_" + name)), per, credit)

        y = sb("y", [P, KT, N])
        a = sb("a", [P, KT, N])
        x1 = sb("x1", [P, CT, N])
        f_all = sb("f_all", [P, KT, N], F32R)
        q_all = pooled.shared
        pooled.other = f_all
        v_all = sb("v_all", [P, KT, N], F32R)
        pt_all = sb("pt_all", [P, KT, N], F32R)
        f_hi, f_lo = f_all[:, 0:CT], f_all[:, CT:KT]
        q_hi, q_lo = q_all[:, 0:CT], q_all[:, CT:KT]
        v_hi, v_lo = (v_all[:, k:k + CT].rearrange("p t (m c) -> p (t m) c", c=C) for k in (0, CT))
        pt_hi, pt_lo = pt_all[:, 0:2], pt_all[:, 2:4]
        a_hi, a_lo, y_hi, y_lo = f_all, q_all, v_all, pt_all
        prob = chain.stem
        mixed = sb("mixed", [P, 2, C])
        minus_max = sb("c_minus_max", [P, TILES])
        row_sum = sb("row_sum", [P, TILES])
        row_inv = sb("row_inv", [P, TILES])
        stats = sb("c_stats", [P, CT, 2, 6])
        mv = sb("c_mv", [P, CT, 2])
        gmean = sb("gmean", [P, CT])
        dev = sb("c_dev", [P, CT])
        spread = sb("c_spread", [P, CT])
        rstd = sb("c_rstd", [P, CT])
        shift = sb("c_shift", [P, CT])
        slots = [ctx.enter_context(nc.psum_tensor(f"slot{n}", [P, N], F32)) for n in range(3)]
        ps_o = ctx.enter_context(nc.psum_tensor("ps_o", [P, HALF], F32))
        ps_ot = ctx.enter_context(nc.psum_tensor("ps_ot", [P, HALF], F32))

        x_loaded = signal("x_loaded", 16)
        stored = signal("stored", 16)
        cv = signal("cv", 2 * CT)
        y_ready = signal("y_ready", KT)
        taps_centre = signal("taps_centre", KT * STAGES)
        taps = signal("taps", 2 * KT * STAGES)
        a_hi_done = signal("a_hi", KT)
        a_lo_done = signal("a_lo", KT)
        c1 = signal("c1", KT)
        gated = signal("gated", KT)
        y_hi_done = signal("y_hi", KT)
        y_lo_done = signal("y_lo", KT)
        cvend = signal("cvend", CT)
        ended = signal("ended", CT)
        added = signal("added", CT)
        bn = signal("bn", 4 + CT)
        group_mean = signal("group_mean", 1)
        group_var = signal("group_var", 1)
        norm = signal("norm", 6)
        rstd_done = signal("rstd", 1)
        f_done = signal("f", CT)
        f_hi_done = signal("f_hi", CT)
        f_lo_done = signal("f_lo", CT)
        qv = signal("qv", 4)
        qv_hi = signal("qv_hi", 4)
        qv_lo = signal("qv_lo", 4)
        scores = signal("scores", TILES)
        maxed = signal("maxed", TILES)
        prob_done = signal("prob", TILES)
        turned = signal("turned", TILES, credit=TILES)
        pt_hi_done = signal("pt_hi", TILES)
        pt_lo_done = signal("pt_lo", TILES)
        pv = signal("pv", TILES)
        inverse = signal("inverse", TILES)
        mixed_done = signal("mixed", TILES)
        back = signal("back", TILES)
        result = signal("result", TILES)
        stats_gate = ctx.enter_context(nc.semaphore("c_gate"))
        block = ctx.enter_context(nc.Block())

        x_v = x.rearrange("b (t p) h w -> b p t (h w)", p=P)
        out_v = out.rearrange("b (t p) h w -> b p t (h w)", p=P)

        def steps(eng, step):
            step(0, True, False, True)
            with eng.Fori(1, B - 1) as i:
                step(i, True, True, True)
            step(B - 1, True, True, False)
            step(B, False, True, False)

        def slot_uses(conv, attn):
            uses = [("cv", k) for k in range(2 * CT)] if conv else []
            if attn:
                uses += [("qv", k) for k in range(4)] + [("s", 0)]
                for t in range(TILES):
                    uses += [("s", t + 1)] * (t + 1 < TILES) + [("t", t)]
            return uses + ([("c1", k) for k in range(KT)] + [("ce", k) for k in range(CT)] if conv else [])

        def slot_plan(conv, attn):
            first = 1 if attn else 0
            return {use: slots[(first + n) % 3] for n, use in enumerate(slot_uses(conv, attn))}

        def schedule(attn):
            if attn:
                return [(c + u, s) for c in range(0, KT, 2) for s in range(STAGES) for u in range(2)]
            return [(0, 0), (0, 1), (1, 0), (0, 2), (1, 1), (0, 3), (1, 2), (2, 0),
                    (1, 3), (2, 1), (3, 0), (2, 2), (3, 1), (2, 3), (3, 2), (3, 3)]

        def stage(n, attn):
            c, s = schedule(attn)[n]
            between = chain.work_b[:, :] if c % 2 else chain.work_a[:, 0:N]
            c = ORDER[c]
            src, dst = ((y[:, c], between), (between, a[:, c]), (a[:, c], between), (between, a[:, c]))[s]
            return c, s, src, dst

        def finished(c, s, attn):
            return 2 * schedule(attn).index((c, s)) + 2

        def wait_before(eng, i, n, attn):
            c, s = schedule(attn)[n]
            if s:
                wait(eng, taps, i, finished(c, s - 1, attn))
            else:
                wait(eng, y_ready, i, c + 1)
                if c > 1:
                    wait(eng, taps, i, finished(c - 2, STAGES - 1, attn))
                else:
                    wait(eng, chain.done, i, MIX * LEVELS)

        @block.sync
        def _(sp):
            def load_chain(i):
                sp.dma_start(chain.stem[:, :], levels[i]).then_inc(chain.loaded.sem, 16)

            def step(i, conv, attn, chained):
                if chained:
                    wait(sp, chain.padded, i, 2)
                    if attn:
                        wait(sp, turned, i - 2, TILES)
                    load_chain(i + 1)
                    wait(sp, pooled.lo_done, i, 2)
                    pooled.load_second(sp, i + 1)
                if attn:
                    wait(sp, result, i - 1, TILES)
                    sp.dma_start(out_v[i - 1], x1[:, :, :]).then_inc(stored.sem, 16)
                    wait(sp, stored, i - 1, 16)
                if conv:
                    sp.dma_start(x1[:, :, :], x_v[i]).then_inc(x_loaded.sem, 16)
                if chained:
                    wait(sp, c1, i, KT)
                    pooled.load_others(sp, i + 1)

            for u in range(2):
                sp.wait_ge(pooled.stored[u], 16 * (B // 2) * (LEVELS + 1))
            steps(sp, step)

        @block.gpsimd
        def _(pool):
            def inputs_lo(i, n):
                k = ORDER[n]
                wait(pool, a_hi_done, i, n + 1)
                nc.gpsimd.tensor_tensor(a_lo[:, k], a[:, k], a_hi[:, k].bitcast(F32), ALU.subtract).then_inc(a_lo_done.sem, 1)

            def box_sums(i, level):
                chain.box_sums_start(pool, i, level)
                chain.box_sums_end(pool, i, level)

            def step(i, conv, attn, chained):
                if attn:
                    wait(pool, norm, i - 1, 4)
                    nc.gpsimd.tensor_tensor(rstd[:, :], spread[:, :], keep["minus_half"][:, 0:CT], ALU.pow).then_inc(rstd_done.sem, 1)
                if attn and conv:
                    for t in range(CT):
                        wait(pool, f_hi_done, i - 1, t + 1)
                        nc.gpsimd.tensor_tensor(f_lo[:, t], a[:, t], f_hi[:, t].bitcast(F32), ALU.subtract).then_inc(f_lo_done.sem, 1)
                if chained:
                    wait(pool, chain.done, i, MIX * LEVELS)
                if chained and attn:
                    box_sums(i + 1, 0)
                if conv:
                    for n in range(KT):
                        inputs_lo(i, n)
                        if not attn and n == 0:
                            chain.box_sums_start(pool, i + 1, 0)
                        if not attn and n == 1:
                            chain.box_sums_end(pool, i + 1, 0)
                if chained:
                    box_sums(i + 1, 1)
                    box_sums(i + 1, 2)

            steps(pool, step)

        @block.tensor
        def _(pe):
            def released(use, i, own):
                kind, k = use
                image = i if own else i - 1
                return {"cv": (y_ready, image, k + 1), "c1": (gated, image, k + 1), "ce": (ended, image, k + 1),
                        "qv": (qv_lo, i - 1, k + 1), "s": (prob_done, i - 1, k + 1), "t": (pt_lo_done, i - 1, k + 1)}[kind]

            def step(i, conv, attn, chained):
                uses, slots_of = slot_uses(conv, attn), slot_plan(conv, attn)

                def claim(kind, k):
                    n = uses.index((kind, k))
                    if n >= 3:
                        wait(pe, *released(uses[n - 3], i, True))
                    elif attn:
                        wait(pe, *released(slot_uses(True, False)[n - 3], i, False))
                    return slots_of[kind, k]

                def cv1(m, between=None):
                    slot = claim("cv", CT + m)
                    for h in range(2):
                        for k in range(KT):
                            if m == 0 and h == 0 and k:
                                wait(pe, chain.done, i, MIX * k)
                            rows = chain.wide[:, k, h * (H // 2):(h + 1) * (H // 2), 2:2 + W]
                            last = nc.tensor.matmul(slot[:, h * HALF:(h + 1) * HALF], keep["cv1"][:, k, cols(m)], rows,
                                                    start=(k == 0), stop=(k == KT - 1))
                        if h == 0 and between:
                            between()
                    last.then_inc(cv.sem, 1)

                def cols(m):
                    return slice(m * P, (m + 1) * P)

                def product_split(kind, m, name, hi, lo, sig, order, hi_ready, lo_ready):
                    slot = claim(kind, m)
                    w_hi, w_lo = keep[name + "_hi"][:, :, cols(m)], keep[name + "_lo"][:, :, cols(m)]
                    parts = ((w_hi, hi, hi_ready), (w_lo, hi, hi_ready), (w_hi, lo, lo_ready))
                    uses = [(n, part) for part in parts for n in range(KT - 1)] + [(KT - 1, part) for part in parts]
                    for at, (n, (weights, inputs, ready)) in enumerate(uses):
                        k = order[n]
                        if m == 0:
                            ready(n)
                        for h in range(2):
                            hs = slice(h * HALF, (h + 1) * HALF)
                            last = nc.tensor.matmul(slot[:, hs], weights[:, k], inputs(k)[:, hs],
                                                    start=(at == 0), stop=(at == len(uses) - 1))
                    last.then_inc(sig.sem, 1)

                def tiles_of(t):
                    return lambda k: t[:, k]

                def when(sig):
                    return lambda n: wait(pe, sig, i, n + 1)

                def cv2(m):
                    product_split("cv", m, "cv2", pooled.hi, pooled.lo, cv, pooled.ORDER, when(pooled.hi_done),
                                  when(pooled.lo_done))

                def c1_alone():
                    ms = range(KT - 1)
                    slot = [claim("c1", m) for m in ms]
                    for n, k in enumerate(ORDER):
                        for part, (name, inputs, done) in enumerate((("c1_hi", a_hi, a_hi_done), ("c1_lo", a_hi, a_hi_done),
                                                                     ("c1_hi", a_lo, a_lo_done))):
                            wait(pe, done, i, n + 1)
                            for m in ms:
                                for h in range(2):
                                    hs = slice(h * HALF, (h + 1) * HALF)
                                    last = nc.tensor.matmul(slot[m][:, hs], keep[name][:, k, cols(m)], inputs[:, k, hs],
                                                            start=(n == 0 and part == 0), stop=(n == KT - 1 and part == 2))
                                if n == KT - 1 and part == 2:
                                    last.then_inc(c1.sem, 1)

                def split_product(out, pairs, lo_ready=None):
                    parts = [(lh, rh) for lh, ll, rh, rl in pairs] + [(ll, rh) for lh, ll, rh, rl in pairs] \
                        + [(lh, rl) for lh, ll, rh, rl in pairs]
                    for n, (lhs, rhs) in enumerate(parts):
                        if n == 2 * len(pairs) and lo_ready:
                            lo_ready()
                        last = nc.tensor.matmul(out, lhs, rhs, start=(n == 0), stop=(n == len(parts) - 1))
                    return last

                def score(t):
                    wait(pe, qv_lo, i - 1, 2)
                    slot = claim("s", t)
                    for h in range(2):
                        hs = slice(h * HALF, (h + 1) * HALF)
                        last = split_product(slot[:, hs], [(q_hi[:, k, cols(t)], q_lo[:, k, cols(t)], f_hi[:, k, hs], f_lo[:, k, hs])
                                                           for k in range(CT)])
                    last.then_inc(scores.sem, 1)

                def turn(t):
                    wait(pe, prob_done, i - 1, t + 1)
                    slot = claim("t", t)
                    for m in range(N // P):
                        last = nc.tensor.transpose(slot[:, cols(m)], prob[:, cols(m)], keep["ident"][:, :])
                    last.then_inc(turned.sem, 1)

                def mix(t):
                    wait(pe, pt_lo_done, i - 1, t + 1)
                    wait(pe, qv_lo, i - 1, 4)
                    if t:
                        wait(pe, mixed_done, i - 1, t)
                    split_product(ps_o[:, 0:C], [(pt_hi[:, t % 2, cols(m)], pt_lo[:, t % 2, cols(m)], v_hi[:, m], v_lo[:, m])
                                                 for m in range(N // P)]).then_inc(pv.sem, 1)

                def turn_back(t):
                    wait(pe, mixed_done, i - 1, t + 1)
                    if t:
                        wait(pe, result, i - 1, t)
                    for d in range(CT):
                        last = nc.tensor.transpose(ps_ot[:, cols(d)], mixed[:, t % 2, cols(d)], keep["ident"][:, :])
                    last.then_inc(back.sem, 1)

                def group_sums(rhs, ps, sig):
                    nc.tensor.matmul(ps[:, 0:CT], keep["group"][:, :], rhs, start=True, stop=True).then_inc(sig.sem, 1)

                def means():
                    wait(pe, bn, i - 1, 4 + CT)
                    group_sums(mv[:, :, 0], ps_o, group_mean)

                def variances():
                    wait(pe, norm, i - 1, 3)
                    group_sums(spread[:, :], ps_ot, group_var)

                if conv:
                    cv2(0)
                    cv2(1)
                    wait(pe, chain.padded, i, 1)
                    cv1(0, between=means if attn else None)
                elif attn:
                    means()
                if attn:
                    variances()
                if conv:
                    cv1(1)
                if attn:
                    wait(pe, f_hi_done, i - 1, CT)
                    for m in range(CT):
                        slot = claim("qv", m)
                        for h in range(2):
                            hs = slice(h * HALF, (h + 1) * HALF)
                            last = split_product(slot[:, hs], [(keep["w1_hi"][:, k, cols(m)], keep["w1_lo"][:, k, cols(m)],
                                                                f_hi[:, k, hs], f_lo[:, k, hs]) for k in range(CT)],
                                                 lo_ready=lambda: wait(pe, f_lo_done, i - 1, CT))
                        last.then_inc(qv.sem, 1)
                    for half in range(2):
                        slot = claim("qv", 2 + half)
                        for m in range(4):
                            px = cols(4 * half + m)
                            last = split_product(slot[:, m * C:(m + 1) * C], [(f_hi[:, k, px], f_lo[:, k, px], keep["w2_hi"][:, k],
                                                                              keep["w2_lo"][:, k]) for k in range(CT)])
                        last.then_inc(qv.sem, 1)
                    score(0)
                    for t in range(TILES):
                        if t + 1 < TILES:
                            score(t + 1)
                        if t > 1:
                            turn_back(t - 2)
                        if t and t + 1 < TILES:
                            mix(t - 1)
                        turn(t)
                    for t in range(TILES - 2, TILES):
                        mix(t)
                    turn_back(TILES - 2)
                    if not conv:
                        turn_back(TILES - 1)
                if conv:
                    if not attn:
                        c1_alone()
                    for m in range(0 if attn else KT - 1, KT):
                        product_split("c1", m, "c1", tiles_of(a_hi), tiles_of(a_lo), c1, ORDER, when(a_hi_done), when(a_lo_done))
                        if attn and m == 0:
                            turn_back(TILES - 1)
                    for m in range(CT):
                        product_split("ce", m, "cvend", tiles_of(y_hi), tiles_of(y_lo), cvend, range(KT), when(y_hi_done), when(y_lo_done))

            pe.sem_inc(turned.sem, TILES)
            steps(pe, step)

        @block.scalar
        def _(act):
            def step(i, conv, attn, chained):
                def silu_cv(k):
                    c = ORDER[k]
                    wait(act, cv, i, k + 1)
                    bias = keep["b_cv1"][:, c:c + 1] if c < CT else keep["b_cv2"][:, c - CT:c - CT + 1]
                    nc.scalar.activation(y[:, c], slots_of["cv", k][:, :], ACT.Silu, bias=bias).then_inc(y_ready.sem, 1)

                def centre_tap(n):
                    c, s, src, dst = stage(n, attn)
                    wait_before(act, i, n, attn)
                    if attn and schedule(attn)[n] == (2, 1):
                        wait(act, f_lo_done, i - 1, CT)
                    nc.scalar.activation(dst, src, ACT.Identity, scale=keep["taps"][:, s, c, 1:2],
                                         bias=keep["b_taps"][:, s, c:c + 1]).then_inc(taps_centre.sem, 1)

                def exponent(t):
                    wait(act, maxed, i - 1, t + 1)
                    if t:
                        wait(act, turned, i - 1, t)
                    elif chained:
                        wait(act, chain.padded, i + 1, 2)
                    nc.scalar.activation(prob[:, :], slots_of["s", t][:, :], ACT.Exp, bias=minus_max[:, t:t + 1],
                                         accum_out=row_sum[:, t:t + 1]).then_inc(prob_done.sem, 1)

                def turned_hi(t):
                    wait(act, turned, i - 1, t + 1)
                    nc.scalar.copy(pt_hi[:, t % 2], slots_of["t", t][:, :]).then_inc(pt_hi_done.sem, 1)

                def inputs_hi(n):
                    wait(act, taps, i, finished(n, STAGES - 1, attn))
                    nc.scalar.copy(a_hi[:, ORDER[n]], a[:, ORDER[n]]).then_inc(a_hi_done.sem, 1)

                def gated_hi(m):
                    wait(act, gated, i, m + 1)
                    nc.scalar.copy(y_hi[:, m], y[:, m]).then_inc(y_hi_done.sem, 1)

                def scale_mixed(t):
                    wait(act, pv, i - 1, t + 1)
                    wait(act, inverse, i - 1, t + 1)
                    nc.scalar.activation(mixed[:, t % 2], ps_o[:, 0:C], ACT.Copy, scale=row_inv[:, t:t + 1]).then_inc(mixed_done.sem, 1)

                slots_of = slot_plan(conv, attn)
                if conv and not attn:
                    for n, (c, s) in enumerate(schedule(attn)):
                        if s == 0:
                            silu_cv(c)
                        centre_tap(n)
                        if (c, s) == (KT - 1, 0):
                            chain.pad_first(act, i + 1)
                        if s == STAGES - 1 and c:
                            inputs_hi(c - 1)
                elif conv:
                    for n in range(CT):
                        silu_cv(n)
                    for n in range(3):
                        centre_tap(n)
                    silu_cv(2)
                if attn:
                    for t in range(CT):
                        wait(act, norm, i - 1, 6)
                        nc.scalar.activation(a[:, t], x1[:, t], ACT.Identity, scale=rstd[:, t:t + 1],
                                             bias=shift[:, t:t + 1]).then_inc(f_done.sem, 1)
                        wait(act, f_done, i - 1, t + 1)
                        nc.scalar.copy(f_hi[:, t], a[:, t]).then_inc(f_hi_done.sem, 1)
                if conv and attn:
                    for n in range(3, BEFORE - 2):
                        centre_tap(n)
                    silu_cv(3)
                    centre_tap(BEFORE - 2)
                if attn:
                    for k in range(4):
                        wait(act, qv, i - 1, k + 1)
                        src = slots_of["qv", k][:, :]
                        if k < 2:
                            nc.scalar.activation(q_hi[:, k], src, ACT.Copy, scale=C ** -0.5).then_inc(qv_hi.sem, 1)
                        else:
                            nc.scalar.copy(v_all[:, k - 2], src).then_inc(qv_hi.sem, 1)
                        if k == 2:
                            nc.scalar.preload_act_table_set(EXP_LN)
                        if conv and k == 1:
                            centre_tap(BEFORE - 1)
                if chained and attn:
                    wait(act, cv, i, 2 * CT)
                    chain.pad_first(act, i + 1)
                if attn:
                    if conv:
                        centre_tap(BEFORE)
                    for t in range(TILES):
                        if t > 1:
                            scale_mixed(t - 2)
                        if t:
                            turned_hi(t - 1)
                        if t == 1 and conv:
                            centre_tap(BEFORE + 1)
                        exponent(t)
                        if t == TILES - 1:
                            turned_hi(t)
                        if conv and t and BEFORE + t + 1 < KT * STAGES:
                            centre_tap(BEFORE + t + 1)
                    if conv:
                        inputs_hi(0)
                        inputs_hi(1)
                    scale_mixed(TILES - 2)
                    if conv:
                        inputs_hi(2)
                    scale_mixed(TILES - 1)
                if conv:
                    inputs_hi(KT - 1)
                if chained:
                    chain.average(act, i + 1, 0)
                    chain.pad_next(act, i + 1, 1)
                if conv:
                    for m in range(KT - 1):
                        gated_hi(m)
                    if not attn:
                        gated_hi(KT - 1)
                if chained:
                    chain.average(act, i + 1, 1)
                if conv and attn:
                    gated_hi(KT - 1)
                if chained:
                    chain.pad_next(act, i + 1, 2)
                    wait(act, c1, i, KT)
                    pooled.split_hi(act, i + 1, 0)
                    pooled.split_hi(act, i + 1, 1)
                if conv:
                    for m in range(CT):
                        wait(act, cvend, i, m + 1)
                        nc.scalar.activation(a[:, m], slots_of["ce", m][:, :], ACT.Silu, bias=keep["b_cvend"][:, m:m + 1]).then_inc(ended.sem, 1)
                        if chained and m == 0:
                            pooled.split_hi(act, i + 1, 2)
                            pooled.split_hi(act, i + 1, 3)
                if chained:
                    chain.average(act, i + 1, LEVELS - 1)

            for n in range(KT):
                pooled.split_hi(act, 0, n)
            steps(act, step)

        @block.vector
        def _(dve):
            def step(i, conv, attn, chained):
                def outer_taps(n):
                    c, s, src, dst = stage(n, attn)
                    wait(dve, taps_centre, i, n + 1)
                    src, dst = image2d(src), image2d(dst)
                    d = 1 if s < 2 else 2
                    for k, tap in ((0, 0), (1, 2)):
                        if tap == 0:
                            far, near = slice(d, W), slice(0, W - d)
                        else:
                            far, near = slice(0, W - d), slice(d, W)
                        o, u = (dst[:, :, far], src[:, :, near]) if s % 2 == 0 else (dst[:, far], src[:, near])
                        if k:
                            wait(dve, taps, i, 2 * n + 1)
                        nc.vector.scalar_tensor_tensor(o, u, keep["taps"][:, s, c, tap:tap + 1], o, ALU.mult, ALU.add).then_inc(taps.sem, 1)

                def turned_lo(t):
                    wait(dve, pt_hi_done, i - 1, t + 1)
                    nc.vector.tensor_tensor(pt_lo[:, t % 2], slots_of["t", t][:, :], pt_hi[:, t % 2].bitcast(F32),
                                            ALU.subtract).then_inc(pt_lo_done.sem, 1)

                def maximum(t):
                    wait(dve, scores, i - 1, t + 1)
                    nc.vector.tensor_reduce(minus_max[:, t:t + 1], slots_of["s", t][:, :], AX, ALU.max, negate=True).then_inc(maxed.sem, 1)

                def invert(t):
                    wait(dve, prob_done, i - 1, t + 1)
                    nc.vector.reciprocal(row_inv[:, t:t + 1], row_sum[:, t:t + 1]).then_inc(inverse.sem, 1)

                def add_attention(t):
                    wait(dve, back, i - 1, t + 1)
                    part = x1[:, :, t * P:(t + 1) * P]
                    nc.vector.tensor_tensor(part, ps_ot[:, 0:C].rearrange("p (d n) -> p d n", d=CT), part, ALU.add).then_inc(result.sem, 1)

                def gate(m):
                    wait(dve, c1, i, m + 1)
                    nc.vector.scalar_tensor_tensor(y[:, m], slots_of["c1", m][:, :], keep["b_c1"][:, m:m + 1], y[:, m],
                                                   ALU.add, ALU.mult).then_inc(gated.sem, 1)

                def gated_lo(m):
                    wait(dve, y_hi_done, i, m + 1)
                    nc.vector.tensor_tensor(y_lo[:, m], y[:, m], y_hi[:, m].bitcast(F32), ALU.subtract).then_inc(y_lo_done.sem, 1)

                def add_l0(m):
                    wait(dve, x_loaded, i, 16)
                    wait(dve, ended, i, m + 1)
                    nc.vector.tensor_tensor(x1[:, m], a[:, m], x1[:, m], ALU.add).then_inc(added.sem, 1)
                    wait(dve, added, i, m + 1)
                    for h in range(2):
                        nc.vector.bn_stats(stats[:, m, h, :], x1[:, m, h * HALF:(h + 1) * HALF]).then_inc(bn.sem, 1)

                slots_of = slot_plan(conv, attn)
                before = iter(range(BEFORE if attn else KT * STAGES))
                if attn:
                    small = Steps(dve, norm, i - 1)
                    wait(dve, group_mean, i - 1, 1)
                    small.did(nc.vector.tensor_tensor(dev[:, :], mv[:, :, 0], ps_o[:, 0:CT], ALU.subtract))
                    small.wait()
                    small.did(nc.vector.tensor_tensor(dev[:, :], dev[:, :], dev[:, :], ALU.mult))
                    small.wait()
                    small.did(nc.vector.tensor_tensor(spread[:, :], dev[:, :], mv[:, :, 1], ALU.add))
                if conv:
                    outer_taps(next(before))
                if attn:
                    wait(dve, group_var, i - 1, 1)
                    small.did(nc.vector.tensor_scalar(spread[:, :], ps_ot[:, 0:CT], 1e-5, None, ALU.add))
                    small.did(nc.vector.tensor_scalar(gmean[:, :], ps_o[:, 0:CT], -1.0, None, ALU.mult))
                    small.wait()
                    wait(dve, rstd_done, i - 1, 1)
                    small.did(nc.vector.tensor_tensor(shift[:, :], gmean[:, :], rstd[:, :], ALU.mult))
                if conv:
                    outer_taps(next(before))
                if not conv:
                    for t in range(CT):
                        wait(dve, f_hi_done, i - 1, t + 1)
                        nc.vector.tensor_tensor(f_lo[:, t], a[:, t], f_hi[:, t].bitcast(F32), ALU.subtract).then_inc(f_lo_done.sem, 1)
                if conv:
                    for n in before:
                        outer_taps(n)
                        if attn and n == BEFORE - 3:
                            break
                if attn:
                    for k in range(4):
                        if conv and k == 2:
                            outer_taps(next(before))
                        wait(dve, qv_hi, i - 1, k + 1)
                        src = slots_of["qv", k][:, :]
                        if k < 2:
                            nc.vector.scalar_tensor_tensor(q_lo[:, k], src, C ** -0.5, q_hi[:, k].bitcast(F32),
                                                           ALU.mult, ALU.subtract).then_inc(qv_lo.sem, 1)
                        else:
                            nc.vector.tensor_tensor(v_all[:, CT + k - 2], src, v_all[:, k - 2].bitcast(F32),
                                                    ALU.subtract).then_inc(qv_lo.sem, 1)
                    maximum(0)
                    if conv:
                        outer_taps(BEFORE - 1)
                    for t in range(TILES):
                        if t:
                            turned_lo(t - 1)
                        if conv and t == 1:
                            outer_taps(BEFORE)
                        if conv and t:
                            outer_taps(BEFORE + t)
                        if t + 1 < TILES:
                            maximum(t + 1)
                        invert(t)
                        if t > 1:
                            add_attention(t - 2)
                    turned_lo(TILES - 1)
                if chained:
                    wait(dve, taps, i, 2 * KT * STAGES)
                    chain.row_maxima(dve, i + 1, 0)
                if attn:
                    add_attention(TILES - 2)
                if chained:
                    chain.column_maxima(dve, i + 1, 0)
                if chained:
                    chain.mixture(dve, i + 1, 0)
                if conv:
                    gate(0)
                if attn:
                    add_attention(TILES - 1)
                if chained and attn:
                    chain.row_maxima(dve, i + 1, 1)
                if conv:
                    gate(1)
                    gated_lo(0)
                if chained and attn:
                    chain.column_maxima(dve, i + 1, 1)
                if conv:
                    gate(2)
                    gated_lo(1)
                    gate(3)
                    if not attn:
                        gated_lo(2)
                        gated_lo(3)
                if chained and not attn:
                    chain.maxima(dve, i + 1, 1)
                if chained:
                    chain.mixture(dve, i + 1, 1)
                if conv and attn:
                    gated_lo(2)
                    gated_lo(3)
                if chained:
                    pooled.split_lo(dve, i + 1, 0)
                    pooled.split_lo(dve, i + 1, 1)
                    chain.row_maxima(dve, i + 1, 2)
                    pooled.split_lo(dve, i + 1, 2)
                    pooled.split_lo(dve, i + 1, 3)
                if conv:
                    add_l0(0)
                if chained:
                    chain.column_maxima(dve, i + 1, 2)
                    chain.mixture(dve, i + 1, 2)
                if conv:
                    add_l0(1)
                    wait(dve, bn, i, 4)
                    dve.sem_inc(stats_gate, 1)
                    for m in range(CT):
                        nc.vector.bn_aggr(mv[:, m, :], stats[:, m].rearrange("p h s -> p (h s)")).then_inc(bn.sem, 1)

            for n in range(KT):
                pooled.split_lo(dve, 0, n)
            steps(dve, step)


def program(nc, x, w, consts, levels, out):
    with ExitStack() as ctx:
        keep = kept_tensors(ctx, nc)
        chain = Chain(ctx, nc)
        pooled = Pooled(ctx, nc, levels, chain)
        with ExitStack() as stem_and_levels:
            box = stem_and_levels.enter_context(nc.sbuf_tensor("box", [P, 8 * W], F32R))
            rmc = stem_and_levels.enter_context(nc.sbuf_tensor("rmc", [P, B], F32))
            phase_a(nc, x, w, consts, keep, levels, rmc, box, chain, pooled)
            phase_b(nc, keep, levels, rmc, box, chain, pooled)
        phase_c(nc, x, out, keep, levels, chain, pooled)


def kernel(**inputs):
    import numpy as np
    import concourse.bacc as bacc
    from concourse.bass_utils import run_bass_kernel_spmd

    nc = bacc.Bacc("TRN2", target_bir_lowering=False, num_devices=1)
    arrays = {"x": np.ascontiguousarray(inputs["x"]), "columns": columns(inputs)}
    for k in ("sta", "cv1", "cv2", "cvend", "c1"):
        arrays["w_" + k] = np.ascontiguousarray(inputs["L0_conv_w_" + k][:, :, 0, 0].T)
    for k in ("w1", "w2"):
        arrays["w_" + k] = np.ascontiguousarray(inputs["L1_conv_" + k].T)
    for k, v in constants().items():
        arrays["const_" + k] = v
    aps = {k: nc.dram_tensor("in_" + k, v.shape, F32, kind="ExternalInput").ap() for k, v in arrays.items()}
    levels = nc.dram_tensor("levels", ((LEVELS + 1) * B, P, N), F32, kind="Internal").ap()
    out = nc.dram_tensor("out", (B, C, H, W), F32, kind="ExternalOutput").ap()
    w = {k[2:]: v for k, v in aps.items() if k.startswith("w_")}
    w["columns"] = aps["columns"]
    consts = {k[6:]: v for k, v in aps.items() if k.startswith("const_")}
    program(nc, aps["x"], w, consts, levels, out)
    r = run_bass_kernel_spmd(nc, [{"in_" + k: v for k, v in arrays.items()}], core_ids=[0])
    return r.results[0]["out"]
```
